# Optimizing a Trainium2 kernel written in Bass

```python
import numpy as np
import jax
import jax.numpy as jnp

def _softmax(x, axis=-1):
    return jax.nn.softmax(x, axis=axis)

def _gelu(x):
    return jax.nn.gelu(x, approximate=True)

def _silu(x):
    return jax.nn.silu(x)

def _sigmoid(x):
    return jax.nn.sigmoid(x)

def _layernorm(x, axis=-1, eps=1e-05):
    m = jnp.mean(x, axis=axis, keepdims=True)
    v = jnp.var(x, axis=axis, keepdims=True)
    return (x - m) / jnp.sqrt(v + eps)

def _scatter_add(tgt, idx, src, axis=0):
    return tgt.at[idx].add(src)

def _segment_sum(src, seg, n):
    return jax.ops.segment_sum(src, seg, n)
kernel_name = 'mk_dlrm_tower_d1_rec_r8_a0dd41'

def setup_inputs(seed: int=0):
    np.random.seed(seed)
    _w = jnp.asarray

    def _rec_inputs():
        import jax
        import jax.numpy as jnp
        _tk = jax.random.key(seed)
        ids = jnp.stack([jax.random.randint(jax.random.fold_in(_tk, 200 + f), (2048,), 0, v, jnp.int32) for f, v in enumerate([1000, 1000, 1250, 1000, 1250, 125000, 1250, 1000, 12500, 1250, 1000, 1250, 125000, 1000, 1000, 1250, 12500, 125000, 1000, 12500, 1250, 1000, 1000, 1250, 1000, 1250])], axis=1)
        tbl_0 = 0.05 * jax.random.normal(jax.random.fold_in(_tk, 500 + 0), (1000, 64), jnp.float32)
        tbl_1 = 0.05 * jax.random.normal(jax.random.fold_in(_tk, 500 + 1), (1000, 64), jnp.float32)
        tbl_2 = 0.05 * jax.random.normal(jax.random.fold_in(_tk, 500 + 2), (1250, 64), jnp.float32)
        tbl_3 = 0.05 * jax.random.normal(jax.random.fold_in(_tk, 500 + 3), (1000, 64), jnp.float32)
        tbl_4 = 0.05 * jax.random.normal(jax.random.fold_in(_tk, 500 + 4), (1250, 64), jnp.float32)
        tbl_5 = 0.05 * jax.random.normal(jax.random.fold_in(_tk, 500 + 5), (125000, 64), jnp.float32)
        tbl_6 = 0.05 * jax.random.normal(jax.random.fold_in(_tk, 500 + 6), (1250, 64), jnp.float32)
        tbl_7 = 0.05 * jax.random.normal(jax.random.fold_in(_tk, 500 + 7), (1000, 64), jnp.float32)
        tbl_8 = 0.05 * jax.random.normal(jax.random.fold_in(_tk, 500 + 8), (12500, 64), jnp.float32)
        tbl_9 = 0.05 * jax.random.normal(jax.random.fold_in(_tk, 500 + 9), (1250, 64), jnp.float32)
        tbl_10 = 0.05 * jax.random.normal(jax.random.fold_in(_tk, 500 + 10), (1000, 64), jnp.float32)
        tbl_11 = 0.05 * jax.random.normal(jax.random.fold_in(_tk, 500 + 11), (1250, 64), jnp.float32)
        tbl_12 = 0.05 * jax.random.normal(jax.random.fold_in(_tk, 500 + 12), (125000, 64), jnp.float32)
        tbl_13 = 0.05 * jax.random.normal(jax.random.fold_in(_tk, 500 + 13), (1000, 64), jnp.float32)
        tbl_14 = 0.05 * jax.random.normal(jax.random.fold_in(_tk, 500 + 14), (1000, 64), jnp.float32)
        tbl_15 = 0.05 * jax.random.normal(jax.random.fold_in(_tk, 500 + 15), (1250, 64), jnp.float32)
        tbl_16 = 0.05 * jax.random.normal(jax.random.fold_in(_tk, 500 + 16), (12500, 64), jnp.float32)
        tbl_17 = 0.05 * jax.random.normal(jax.random.fold_in(_tk, 500 + 17), (125000, 64), jnp.float32)
        tbl_18 = 0.05 * jax.random.normal(jax.random.fold_in(_tk, 500 + 18), (1000, 64), jnp.float32)
        tbl_19 = 0.05 * jax.random.normal(jax.random.fold_in(_tk, 500 + 19), (12500, 64), jnp.float32)
        tbl_20 = 0.05 * jax.random.normal(jax.random.fold_in(_tk, 500 + 20), (1250, 64), jnp.float32)
        tbl_21 = 0.05 * jax.random.normal(jax.random.fold_in(_tk, 500 + 21), (1000, 64), jnp.float32)
        tbl_22 = 0.05 * jax.random.normal(jax.random.fold_in(_tk, 500 + 22), (1000, 64), jnp.float32)
        tbl_23 = 0.05 * jax.random.normal(jax.random.fold_in(_tk, 500 + 23), (1250, 64), jnp.float32)
        tbl_24 = 0.05 * jax.random.normal(jax.random.fold_in(_tk, 500 + 24), (1000, 64), jnp.float32)
        tbl_25 = 0.05 * jax.random.normal(jax.random.fold_in(_tk, 500 + 25), (1250, 64), jnp.float32)
        _rk = jax.random.fold_in(_tk, 7)
        r_dense_t = 7.22013e-05 + 1.00017 * jax.random.normal(jax.random.fold_in(_rk, 101), (2048, 256), jnp.float32)
        W_top1 = 0.0360844 * jax.random.normal(jax.random.fold_in(_tk, 801), (768, 512), jnp.float32)
        W_top2 = 0.0441942 * jax.random.normal(jax.random.fold_in(_tk, 802), (512, 256), jnp.float32)
        W_top3 = 0.0625 * jax.random.normal(jax.random.fold_in(_tk, 803), (256, 1), jnp.float32)
        b_top1 = jnp.zeros((512,), jnp.float32)
        b_top2 = jnp.zeros((256,), jnp.float32)
        return (r_dense_t, ids, tbl_0, tbl_1, tbl_2, tbl_3, tbl_4, tbl_5, tbl_6, tbl_7, tbl_8, tbl_9, tbl_10, tbl_11, tbl_12, tbl_13, tbl_14, tbl_15, tbl_16, tbl_17, tbl_18, tbl_19, tbl_20, tbl_21, tbl_22, tbl_23, tbl_24, tbl_25, W_top1, b_top1, W_top2, b_top2, W_top3)
    r_dense_t, ids, tbl_0, tbl_1, tbl_2, tbl_3, tbl_4, tbl_5, tbl_6, tbl_7, tbl_8, tbl_9, tbl_10, tbl_11, tbl_12, tbl_13, tbl_14, tbl_15, tbl_16, tbl_17, tbl_18, tbl_19, tbl_20, tbl_21, tbl_22, tbl_23, tbl_24, tbl_25, W_top1, b_top1, W_top2, b_top2, W_top3 = _rec_inputs()

    def _L0_rec_setup():
        import jax, jax.numpy as jnp
        import numpy as np
        EPS = 1e-05
        NI = 33
        TRIL_I, TRIL_J = np.tril_indices(NI, k=-1)

        def layer_norm(x, g, b):
            m = jnp.mean(x, axis=-1, keepdims=True)
            v = jnp.mean(jnp.square(x - m), axis=-1, keepdims=True)
            return (x - m) * jax.lax.rsqrt(v + EPS) * g + b
        key = jax.random.key(seed)
        ks = jax.random.split(key, 8)
        B, D_DENSE, N_SP, D_SP = (4096, 256, 26, 64)
        E, PROJ, MAXD, NFLAT = (128, 32, 512, 528)
        dense_t = jax.random.normal(ks[0], (B, D_DENSE), dtype=jnp.float32)
        sparse_t = jax.random.normal(ks[1], (B, N_SP, D_SP), dtype=jnp.float32)
        Wd = jax.random.normal(ks[2], (E, D_DENSE), dtype=jnp.float32) / np.sqrt(D_DENSE)
        Ws = jax.random.normal(ks[3], (E, D_SP), dtype=jnp.float32) / np.sqrt(D_SP)
        Wsi = jax.random.normal(ks[4], (PROJ, N_SP), dtype=jnp.float32) / np.sqrt(N_SP)
        Wl = jax.random.normal(ks[5], (MAXD, NFLAT), dtype=jnp.float32) / np.sqrt(NFLAT)
        gd = jnp.ones((E,), jnp.float32)
        bd = jnp.zeros((E,), jnp.float32)
        gs = jnp.ones((E,), jnp.float32)
        bs = jnp.zeros((E,), jnp.float32)
        gsi = jnp.ones((PROJ,), jnp.float32)
        bsi = jnp.zeros((PROJ,), jnp.float32)
        gl = jnp.ones((MAXD,), jnp.float32)
        bl = jnp.zeros((MAXD,), jnp.float32)
        return {'dense_t': dense_t, 'sparse_t': sparse_t, 'Wd': Wd, 'gd': gd, 'bd': bd, 'Ws': Ws, 'gs': gs, 'bs': bs, 'Wsi': Wsi, 'gsi': gsi, 'bsi': bsi, 'Wl': Wl, 'gl': gl, 'bl': bl, 'dims_in_use': 384}
    _L0_rec_all = _L0_rec_setup()
    _L0_rec_in = {k: v for k, v in _L0_rec_all.items() if k in ('Wd', 'gd', 'bd', 'Ws', 'gs', 'bs', 'Wsi', 'gsi', 'bsi', 'Wl', 'gl', 'bl')}
    del _L0_rec_all
    return {'r_dense_t': r_dense_t, 'ids': ids, 'tbl_0': tbl_0, 'tbl_1': tbl_1, 'tbl_2': tbl_2, 'tbl_3': tbl_3, 'tbl_4': tbl_4, 'tbl_5': tbl_5, 'tbl_6': tbl_6, 'tbl_7': tbl_7, 'tbl_8': tbl_8, 'tbl_9': tbl_9, 'tbl_10': tbl_10, 'tbl_11': tbl_11, 'tbl_12': tbl_12, 'tbl_13': tbl_13, 'tbl_14': tbl_14, 'tbl_15': tbl_15, 'tbl_16': tbl_16, 'tbl_17': tbl_17, 'tbl_18': tbl_18, 'tbl_19': tbl_19, 'tbl_20': tbl_20, 'tbl_21': tbl_21, 'tbl_22': tbl_22, 'tbl_23': tbl_23, 'tbl_24': tbl_24, 'tbl_25': tbl_25, 'W_top1': W_top1, 'b_top1': b_top1, 'W_top2': W_top2, 'b_top2': b_top2, 'W_top3': W_top3, 'L0_rec_Wd': _L0_rec_in['Wd'], 'L0_rec_gd': _L0_rec_in['gd'], 'L0_rec_bd': _L0_rec_in['bd'], 'L0_rec_Ws': _L0_rec_in['Ws'], 'L0_rec_gs': _L0_rec_in['gs'], 'L0_rec_bs': _L0_rec_in['bs'], 'L0_rec_Wsi': _L0_rec_in['Wsi'], 'L0_rec_gsi': _L0_rec_in['gsi'], 'L0_rec_bsi': _L0_rec_in['bsi'], 'L0_rec_Wl': _L0_rec_in['Wl'], 'L0_rec_gl': _L0_rec_in['gl'], 'L0_rec_bl': _L0_rec_in['bl']}

def reference(r_dense_t, ids, tbl_0, tbl_1, tbl_2, tbl_3, tbl_4, tbl_5, tbl_6, tbl_7, tbl_8, tbl_9, tbl_10, tbl_11, tbl_12, tbl_13, tbl_14, tbl_15, tbl_16, tbl_17, tbl_18, tbl_19, tbl_20, tbl_21, tbl_22, tbl_23, tbl_24, tbl_25, W_top1, b_top1, W_top2, b_top2, W_top3, L0_rec_Wd, L0_rec_gd, L0_rec_bd, L0_rec_Ws, L0_rec_gs, L0_rec_bs, L0_rec_Wsi, L0_rec_gsi, L0_rec_bsi, L0_rec_Wl, L0_rec_gl, L0_rec_bl):
    import jax
    import jax.numpy as jnp

    def _L0_rec_ref(dense_t, sparse_t, Wd, gd, bd, Ws, gs, bs, Wsi, gsi, bsi, Wl, gl, bl, dims_in_use):
        import jax, jax.numpy as jnp
        import numpy as np
        EPS = 1e-05
        NI = 33
        TRIL_I, TRIL_J = np.tril_indices(NI, k=-1)

        def layer_norm(x, g, b):
            m = jnp.mean(x, axis=-1, keepdims=True)
            v = jnp.mean(jnp.square(x - m), axis=-1, keepdims=True)
            return (x - m) * jax.lax.rsqrt(v + EPS) * g + b
        x = layer_norm(dense_t @ Wd.T, gd, bd)
        y = layer_norm(jnp.einsum('bnd,ed->bne', sparse_t, Ws), gs, bs)
        y = jnp.einsum('bne,pn->bep', y, Wsi)
        y = layer_norm(y, gsi, bsi)
        y = jnp.swapaxes(y, 1, 2)
        T = jnp.concatenate([x[:, None, :], y], axis=1)
        Z = jnp.einsum('bnd,bmd->bnm', T, T)
        Zflat = Z[:, TRIL_I, TRIL_J]
        out = layer_norm(Zflat @ Wl.T, gl, bl)
        maxd = out.shape[-1]
        mask = (jnp.arange(maxd) < dims_in_use).astype(out.dtype)
        return out * mask
    e = jnp.stack([tbl_0[ids[:, 0]], tbl_1[ids[:, 1]], tbl_2[ids[:, 2]], tbl_3[ids[:, 3]], tbl_4[ids[:, 4]], tbl_5[ids[:, 5]], tbl_6[ids[:, 6]], tbl_7[ids[:, 7]], tbl_8[ids[:, 8]], tbl_9[ids[:, 9]], tbl_10[ids[:, 10]], tbl_11[ids[:, 11]], tbl_12[ids[:, 12]], tbl_13[ids[:, 13]], tbl_14[ids[:, 14]], tbl_15[ids[:, 15]], tbl_16[ids[:, 16]], tbl_17[ids[:, 17]], tbl_18[ids[:, 18]], tbl_19[ids[:, 19]], tbl_20[ids[:, 20]], tbl_21[ids[:, 21]], tbl_22[ids[:, 22]], tbl_23[ids[:, 23]], tbl_24[ids[:, 24]], tbl_25[ids[:, 25]]], axis=1)
    z = _L0_rec_ref(r_dense_t, e, L0_rec_Wd, L0_rec_gd, L0_rec_bd, L0_rec_Ws, L0_rec_gs, L0_rec_bs, L0_rec_Wsi, L0_rec_gsi, L0_rec_bsi, L0_rec_Wl, L0_rec_gl, L0_rec_bl, 384)
    z = z.reshape(z.shape[0], -1)
    h = jnp.concatenate([z, r_dense_t], axis=1)
    h = jnp.maximum(h @ W_top1 + b_top1, 0.0)
    h = jnp.maximum(h @ W_top2 + b_top2, 0.0)
    y = h @ W_top3
    return y

_drawn_inputs = setup_inputs


def setup_inputs(seed=0):
    import zlib

    import numpy as np

    out = dict(_drawn_inputs(seed))
    spreads = {'b_top1': (0.0, 0.1),
     'b_top2': (0.0, 0.1),
     'L0_rec_gd': (1.0, 0.6),
     'L0_rec_bd': (0.0, 0.8),
     'L0_rec_gs': (1.0, 0.6),
     'L0_rec_bs': (0.0, 0.1),
     'L0_rec_gsi': (1.0, 0.2),
     'L0_rec_bsi': (0.0, 0.1),
     'L0_rec_gl': (1.0, 0.2),
     'L0_rec_bl': (0.0, 0.1)}
    factors = {}
    for name, (base, spread) in spreads.items():
        noise = np.random.default_rng([zlib.crc32(name.encode()), seed]).standard_normal(out[name].shape)
        drawn = base * np.exp(spread * noise) if base else spread * noise
        out[name] = jnp.asarray(drawn.astype(out[name].dtype))
    for name, factor in factors.items():
        out[name] = (out[name] * factor).astype(out[name].dtype)
    return out
```

```python
from contextlib import ExitStack

import concourse.bass as bass
from concourse import mybir

F32 = mybir.dt.float32
I32 = mybir.dt.int32
ALU = mybir.AluOpType
ACT = mybir.ActivationFunctionType
AX_X = mybir.AxisListType.X

P = 128
BATCH = 2048
N_TABLES = 26
D_SPARSE = 64
D_DENSE = 256
E = 128
PROJ = 32
MAXD = 512
DIMS_IN_USE = 384
TOP1 = 512
TOP2 = 256
EPS = 1e-5

TILES = BATCH // P
QUAD = 4
GROUPS = P // QUAD
CHUNKS = 8
GPC = GROUPS // CHUNKS
SLOTS = GPC * QUAD
ROWS = QUAD * N_TABLES
MIX_K = ROWS + 1
BLOCKS = P * N_TABLES // P // 2
ZCOLS = PROJ + 2
ZQ = 9
EXTRA = 66
CONST_ROW = 64
ZK = DIMS_IN_USE // P
DK = D_DENSE // P
BATCHES = [(0, 4), (4, 7), (7, 10), (10, 13)]
FIRST_PAIR, LAST_PAIR = 0, TILES // 2 - 1
ZS_DMAS = QUAD * QUAD


def at_least(count):
    return max(count, 0) if isinstance(count, int) else count


def columns():
    at, where = 0, {}
    for name, n in (("gp", 1), ("bp", 1), ("gq", 8), ("bq", 8), ("gd", 1), ("bd", 1), ("gl", ZK), ("bl", ZK),
                    ("b1", TOP1 // P), ("b2", TOP2 // P), ("w3", TOP2 // P), ("one", 1)):
        where[name] = (at, at + n)
        at += n
    return where, at


def dlrm_tower(nc, rows, ids, row_offsets, dense, ws, mix, bs_row, gs_rows, wd, wl_pairs, wl_x, delta, ident,
               cols, w1, w2, y):
    where, n_cols = columns()
    with ExitStack() as ctx:
        def sb(name, shape, dt=F32):
            return ctx.enter_context(nc.sbuf_tensor(name, shape, dt))

        def bank(name):
            return ctx.enter_context(nc.psum_tensor(name, [P, 512], F32))

        def sem(name):
            return ctx.enter_context(nc.semaphore(name))

        col = sb("col_sb", [P, n_cols])
        ident_sb = sb("ident_sb", [P, P])
        delta_sb = sb("delta_sb", [P, PROJ])
        offs = sb("offs_sb", [P, N_TABLES])
        ws_sb = sb("ws_sb", [P, 2, E])
        ws_mean = sb("ws_mean", [P, 2])
        mix_sb = sb("mix_sb", [MIX_K, QUAD, PROJ])
        mix_mean = sb("mix_mean", [ROWS, QUAD])
        mix_sum = sb("mix_sum", [1, P])
        gs_sb = sb("gs_sb", [ROWS, E])
        wd_sb = sb("wd_sb", [P, DK, E])
        wl_sb = sb("wl_sb", [P, 8, MAXD])
        wlx_raw = sb("wlx_raw", [PROJ, MAXD])
        wl_extra = sb("wl_extra", [EXTRA, MAXD])
        pair_gain = sb("pair_gain", [P, 8])
        fold = sb("fold", [P, EXTRA])
        fold_q = sb("fold_q", [P, 8, EXTRA])
        fold_x = sb("fold_x", [PROJ, EXTRA])
        w1_sb = sb("w1_sb", [P, ZK + DK, TOP1])
        w2_sb = sb("w2_sb", [P, TOP1 // P, TOP2])
        ones = sb("ones_sb", [P, 1])
        zero_one = sb("zero_one", [P, 2])
        eps = sb("eps_sb", [P, 1])

        ids_raw = sb("ids_raw", [P, 2, N_TABLES], I32)
        idx = sb("idx_sb", [P, 2, N_TABLES], I32)
        emb = [sb(f"emb{b}", [P, BLOCKS, 2, D_SPARSE]) for b in range(2)]
        gate = sb("gate", [1, 2])
        gate_dve = sb("gate_dve", [1, 1])
        emb_t = sb("emb_t", [P, BLOCKS * P])
        y0sq = sb("y0sq", [ROWS, 2, GPC, E])
        ss = sb("ss_sb", [ROWS, 2, GPC])
        sd0 = sb("sd0_sb", [ROWS, 2, GPC])
        r0 = sb("r0_sb", [ROWS, 2, GPC])
        y0s = [sb(f"y0s{b}", [MIX_K, GPC, E]) for b in range(2)]
        y1sq = sb("y1sq", [P, SLOTS, PROJ])
        v1 = sb("v1_sb", [P, SLOTS])
        sd1 = sb("sd1_sb", [P, SLOTS])
        r1 = sb("r1_sb", [P, SLOTS])
        nbuf = [sb(f"nbuf{b}", [P, SLOTS, ZCOLS]) for b in range(2)]
        zt = [sb(f"zt{b}", [P, ZCOLS, GROUPS]) for b in range(2)]
        zs = [sb(f"zs{b}", [P, ZQ, P]) for b in range(2)]
        dense_x = [sb(f"dense_x{b}", [P, DK, P]) for b in range(2)]
        dense_m = sb("dense_m", [P, DK, P])
        x_stats = sb("x_stats", [P, 6])
        x_mv = sb("x_mv", [P, 2])
        x_sd = sb("x_sd", [P, 1])
        x_r = sb("x_r", [P, 1])
        xn = sb("xn_sb", [P, E])
        x_t = [sb(f"x_t{b}", [P, P]) for b in range(2)]
        o_stats = sb("o_stats", [P, 6])
        o_mv = sb("o_mv", [P, 2])
        o_sd = sb("o_sd", [P, 1])
        o_r = sb("o_r", [P, 1])
        zn = sb("zn_sb", [P, DIMS_IN_USE])
        z_t = sb("z_t", [P, ZK, P])
        h1 = sb("h1_sb", [P, TOP1 // P, P])
        h2 = sb("h2_sb", [P, TOP2 // P, P])
        y_rows = sb("y_rows", [1, TILES, P])

        p_emb = bank("p_emb")
        p_y0 = [bank(f"p_y0_{b}") for b in range(2)]
        p_y1 = [bank(f"p_y1_{b}") for b in range(2)]
        p_z = bank("p_z")
        p_out = bank("p_out")
        p_mlp = bank("p_mlp")

        def c(name, i=0, p0=0, p1=P):
            return col[p0:p1, where[name][0] + i:where[name][0] + i + 1]

        weights_in = sem("weights_in")
        late_weights_in = sem("late_weights_in")
        mix_sum_in = sem("mix_sum_in")
        ids_in = [sem(f"ids_in{b}") for b in range(2)]
        idx_ready = sem("idx_ready")
        gate_passed = sem("gate_passed")
        rows_in = [[sem(f"rows_in{b}_{i}") for i in range(BLOCKS)] for b in range(2)]
        emb_tp = sem("emb_tp")
        emb_ready = sem("emb_ready")
        y0_ready = sem("y0_ready")
        ss_ready = sem("ss_ready")
        sd0_ready = sem("sd0_ready")
        r0_ready = sem("r0_ready")
        y0s_ready = sem("y0s_ready")
        y1_ready = sem("y1_ready")
        sq_ready = sem("sq_ready")
        v1_ready = sem("v1_ready")
        sd1_ready = sem("sd1_ready")
        r1_ready = sem("r1_ready")
        n_ready = sem("n_ready")
        z_ready = sem("z_ready")
        zt_ready = sem("zt_ready")
        zs_in = [sem(f"zs_in{b}") for b in range(2)]
        dense_x_in = [sem(f"dense_x_in{b}") for b in range(2)]
        dense_m_in = sem("dense_m_in")
        x_mm = sem("x_mm")
        x_sd_ready = sem("x_sd_ready")
        x_step = sem("x_step")
        xn_ready = sem("xn_ready")
        xt_tp = sem("xt_tp")
        x_ready = sem("x_ready")
        sx_mm = sem("sx_mm")
        sx_ready = sem("sx_ready")
        out_mm = sem("out_mm")
        o_step = sem("o_step")
        o_sd_ready = sem("o_sd_ready")
        zn_ready = sem("zn_ready")
        z_tp = sem("z_tp")
        z_t_ready = sem("z_t_ready")
        top1_mm = sem("top1_mm")
        h1_ready = sem("h1_ready")
        top2_mm = sem("top2_mm")
        h2_ready = sem("h2_ready")
        top3_mm = sem("top3_mm")
        y_ready = sem("y_ready")
        y_out = sem("y_out")
        constants_set = sem("constants_set")
        mean_step = sem("mean_step")
        centred = sem("centred")
        mix_sum_mm = sem("mix_sum_mm")
        mix_sum_ready = sem("mix_sum_ready")
        fold_step = sem("fold_step")
        fold_ready = sem("fold_ready")
        fold_mm = sem("fold_mm")
        wl_ready = sem("wl_ready")
        wl_extra_ready = sem("wl_extra_ready")

        SMALL_LOADS, LATE_LOADS = 9, 5
        block = ctx.enter_context(nc.Block())

        def tile_no(it, b):
            return it * 2 + b

        def exists(t):
            return 0 <= t < TILES if isinstance(t, int) else True

        def is_chunk(s):
            return 0 <= s < TILES * CHUNKS if isinstance(s, int) else True

        def walk(engine, pair):
            pair(FIRST_PAIR)
            with engine.Fori(FIRST_PAIR + 1, LAST_PAIR) as it:
                pair(it)
            pair(LAST_PAIR)
            pair(LAST_PAIR + 1)

        @block.sync
        def _(sp):
            for b in range(2):
                sp.dma_start(ids_raw[:, b, :], ids[b]).then_inc(ids_in[b], 16)
            sp.dma_start(offs[:], row_offsets).then_inc(weights_in, 16)
            sp.dma_start(ws_sb[:], ws).then_inc(weights_in, 16)
            sp.dma_start(ident_sb[:], ident).then_inc(weights_in, 16)
            sp.dma_start(mix_sb[0:ROWS], mix).then_inc(weights_in, 16)
            sp.dma_start(wd_sb[:], wd).then_inc(weights_in, 16)
            sp.dma_start(dense_x[0][:], dense[0]).then_inc(dense_x_in[0], 16)
            sp.dma_start(col[:], cols).then_inc(weights_in, 16)
            sp.dma_start(gs_sb[:], gs_rows).then_inc(weights_in, 16)
            for b in range(2):
                sp.dma_start(y0s[b][ROWS:MIX_K], bs_row).then_inc(weights_in, 16)
            sp.dma_start(delta_sb[:], delta).then_inc(late_weights_in, 16)
            sp.dma_start(wlx_raw[:], wl_x).then_inc(late_weights_in, 16)
            sp.dma_start(wl_sb[:], wl_pairs).then_inc(late_weights_in, 16)
            sp.dma_start(w1_sb[:], w1).then_inc(late_weights_in, 16)
            sp.dma_start(w2_sb[:], w2).then_inc(late_weights_in, 16)
            sp.wait_ge(mix_sum_ready, 1)
            sp.dma_start(mix_sb[ROWS:MIX_K], mix_sum[:].rearrange("o (j p) -> o j p", j=QUAD)).then_inc(mix_sum_in, 16)

            def tile(it, b):
                t = tile_no(it, b)
                if exists(t + 1):
                    sp.wait_ge(x_mm, at_least(t))
                    sp.dma_start(dense_x[1 - b][:], dense[t + 1]).then_inc(dense_x_in[1 - b], 16)
                if exists(t + 2):
                    sp.wait_ge(idx_ready, at_least(t + 1))
                    sp.dma_start(ids_raw[:, b, :], ids[t + 2]).then_inc(ids_in[b], 16)
                if exists(t - 1):
                    sp.wait_ge(zt_ready, at_least(t * CHUNKS))
                    for i in range(QUAD):
                        nq = ZQ if i < 2 else ZQ - 1
                        for j in range(QUAD):
                            sp.dma_start(zs[1 - b][32 * i:32 * i + 32, 0:nq, 32 * j:32 * j + 32],
                                         zt[1 - b][32 * j:32 * j + 32, i:i + 4 * (nq - 1) + 1:4, :]
                                         ).then_inc(zs_in[1 - b], 16)
                    sp.wait_ge(top1_mm, at_least((t - 1) * 2))
                    sp.dma_start(dense_m[:], dense[t - 1]).then_inc(dense_m_in, 16)

            def pair(it):
                for b in range(2):
                    tile(it, b)

            walk(sp, pair)
            sp.wait_ge(y_ready, TILES)
            sp.dma_start(y, y_rows[:]).then_inc(y_out, 16)
            sp.wait_ge(y_out, 16)

        @block.gpsimd
        def _(pool):
            def tile(it, b):
                t = tile_no(it, b)
                if not exists(t):
                    return
                pool.wait_ge(constants_set, 1)
                pool.wait_ge(idx_ready, at_least(t + 1))
                pool.wait_ge(gate_passed, at_least(t))
                nc.gpsimd.tensor_tensor(gate[:, 1:2], gate[:, 0:1], gate[:, 0:1], ALU.add).then_inc(gate_passed, 1)
                for i in range(BLOCKS):
                    for h in range(2):
                        blk = h * BLOCKS + i
                        nc.gpsimd.indirect_dma_start(
                            emb[b][:, i, h, :], None, rows,
                            bass.IndirectOffsetOnAxis(ap=idx[:, b, blk:blk + 1], axis=0),
                        ).then_inc(rows_in[b][i], 16)

            def pair(it):
                for b in range(2):
                    tile(it, b)

            walk(pool, pair)

        @block.tensor
        def _(pe):
            def embed_transposes(t, b, q):
                lo, hi = BATCHES[q]
                pe.wait_ge(emb_ready, at_least(t * 4 + q))
                for i in range(lo, hi):
                    pe.wait_ge(rows_in[b][i], at_least((t - b) * 16 + 32))
                    last = nc.tensor.transpose(p_emb[:, (i - lo) * P:(i - lo + 1) * P],
                                               emb[b][:, i, :, :].rearrange("p h d -> p (h d)"), ident_sb[:])
                last.then_inc(emb_tp, 1)

            def x_matmul(t, b):
                pe.wait_ge(dense_x_in[b], at_least((t - b) * 8 + 16))
                pe.wait_ge(sx_ready, at_least(t))
                for kc in range(DK):
                    last = nc.tensor.matmul(p_mlp[:, 0:E], dense_x[b][:, kc, :], wd_sb[:, kc, :],
                                            start=kc == 0, stop=kc == DK - 1)
                last.then_inc(x_mm, 1)

            def x_transpose(t):
                pe.wait_ge(xn_ready, at_least(t + 1))
                nc.tensor.transpose(p_mlp[:, 0:P], xn[:], ident_sb[:]).then_inc(xt_tp, 1)

            pe.wait_ge(centred, 2)
            nc.tensor.matmul(p_mlp[0:1, 0:P], ones[0:ROWS, :], mix_sb[0:ROWS].rearrange("r j p -> r (j p)"),
                             start=True, stop=True).then_inc(mix_sum_mm, 1)
            pe.wait_ge(weights_in, 16 * SMALL_LOADS)
            pe.wait_ge(mix_sum_ready, 1)
            x_matmul(0, 0)
            x_transpose(0)
            embed_transposes(0, 0, 0)
            pe.wait_ge(late_weights_in, 16 * LATE_LOADS)
            pe.wait_ge(fold_ready, 1)
            for cc in range(8):
                nc.tensor.matmul(p_out[0:EXTRA, :], fold_q[:, cc, :], wl_sb[:, cc, :], start=cc == 0, stop=False)
            nc.tensor.matmul(p_out[0:EXTRA, :], fold_x[:], wlx_raw[:], start=False, stop=True).then_inc(fold_mm, 1)
            pe.wait_ge(mix_sum_in, 16)

            def step(it, b, k):
                t = tile_no(it, b)
                s = t * CHUNKS + k
                if k % 2 == 1 and k < 7 and exists(t):
                    embed_transposes(t, b, (k + 1) // 2)
                if k == 7 and exists(t + 1):
                    embed_transposes(t + 1, 1 - b, 0)
                if is_chunk(s):
                    pe.wait_ge(emb_ready, at_least(t * 4 + k // 2 + 1))
                    pe.wait_ge(y0s_ready, at_least(s - 1))
                    for g2 in range(2):
                        g = 2 * k + g2
                        last = nc.tensor.matmul(p_y0[k % 2][0:ROWS, g2 * 256:(g2 + 1) * 256],
                                                emb_t[:, ROWS * g:ROWS * (g + 1)],
                                                ws_sb[:].rearrange("p h e -> p (h e)"), start=True, stop=True)
                    last.then_inc(y0_ready, 1)
                if is_chunk(s - 1):
                    m = (k - 1) % 2
                    pe.wait_ge(y0s_ready, at_least(s))
                    pe.wait_ge(n_ready, at_least(s - 2))
                    for g in range(GPC):
                        last = nc.tensor.matmul(p_y1[m][:, g * P:(g + 1) * P], y0s[m][:, g, :],
                                                mix_sb[:].rearrange("r j p -> r (j p)"), start=True, stop=True)
                    last.then_inc(y1_ready, 1)
                if is_chunk(s - 2):
                    m = k % 2
                    pe.wait_ge(n_ready, at_least(s - 1))
                    pe.wait_ge(zt_ready, at_least(s - 2))
                    for g in range(GPC):
                        for j in range(QUAD):
                            slot = QUAD * g + j
                            last = nc.tensor.matmul(p_z[32 * j:32 * j + 32, g * ZCOLS:(g + 1) * ZCOLS],
                                                    nbuf[m][:, slot, 0:PROJ], nbuf[m][:, slot, :],
                                                    start=True, stop=True, tile_position=(0, 32 * j))
                    last.then_inc(z_ready, 1)
                if k < 2 and exists(t - 2):
                    if k == 0:
                        pe.wait_ge(z_t_ready, at_least(t - 1))
                        pe.wait_ge(dense_m_in, at_least((t - 1) * 16))
                    for mo in range(2 * k, 2 * k + 2):
                        for kc in range(ZK + DK):
                            act_in = z_t[:, kc, :] if kc < ZK else dense_m[:, kc - ZK, :]
                            last = nc.tensor.matmul(p_mlp[:, mo * P:(mo + 1) * P], w1_sb[:, kc, mo * P:(mo + 1) * P],
                                                    act_in, start=kc == 0, stop=kc == ZK + DK - 1)
                    last.then_inc(top1_mm, 1)
                if k == 2 and exists(t - 2):
                    pe.wait_ge(h1_ready, at_least(t - 1))
                    for mo in range(TOP2 // P):
                        for kc in range(TOP1 // P):
                            last = nc.tensor.matmul(p_mlp[:, mo * P:(mo + 1) * P], w2_sb[:, kc, mo * P:(mo + 1) * P],
                                                    h1[:, kc, :], start=kc == 0, stop=kc == TOP1 // P - 1)
                    last.then_inc(top2_mm, 1)
                if k == 3 and exists(t - 2):
                    pe.wait_ge(h2_ready, at_least(t - 1))
                    for kc in range(TOP2 // P):
                        last = nc.tensor.matmul(p_mlp[0:1, 0:P], c("w3", kc), h2[:, kc, :],
                                                start=kc == 0, stop=kc == TOP2 // P - 1)
                    last.then_inc(top3_mm, 1)
                if k == 4 and exists(t):
                    pe.wait_ge(x_ready, at_least(t + 1))
                    pe.wait_ge(y_ready, at_least(t - 1))
                    nc.tensor.matmul(p_mlp[CONST_ROW:CONST_ROW + 2, 0:P], zero_one[:], x_t[b][:],
                                     start=True, stop=True, tile_position=(0, CONST_ROW)).then_inc(sx_mm, 1)
                if 4 <= k < 7 and exists(t - 1):
                    if k == 4:
                        pe.wait_ge(zs_in[1 - b], at_least((it + b) * (16 * ZS_DMAS)))
                        pe.wait_ge(sx_ready, at_least(t))
                        pe.wait_ge(zn_ready, at_least(t - 1))
                        pe.wait_ge(wl_ready, 1)
                        pe.wait_ge(wl_extra_ready, 1)
                    for cc in range(3 * (k - 4), 3 * (k - 4) + 3):
                        if cc < ZQ - 1:
                            nc.tensor.matmul(p_out[:], zs[1 - b][:, cc, :], wl_sb[:, cc, :],
                                             start=cc == 0, stop=False)
                        else:
                            nc.tensor.matmul(p_out[:], zs[1 - b][0:EXTRA, cc, :], wl_extra[:],
                                             start=False, stop=True).then_inc(out_mm, 1)
                if k == 5 and exists(t + 1):
                    x_matmul(t + 1, 1 - b)
                if k == 6 and exists(t + 1):
                    x_transpose(t + 1)
                if k == 7 and exists(t - 1):
                    pe.wait_ge(zn_ready, at_least(t))
                    if exists(t + 1):
                        pe.wait_ge(x_ready, at_least(t + 2))
                    pe.wait_ge(y_ready, at_least(t - 1))
                    for kc in range(ZK):
                        last = nc.tensor.transpose(p_mlp[:, kc * P:(kc + 1) * P], zn[:, kc * P:(kc + 1) * P],
                                                   ident_sb[:])
                    last.then_inc(z_tp, 1)

            def pair(it):
                for b in range(2):
                    for k in range(CHUNKS):
                        step(it, b, k)

            walk(pe, pair)

        @block.scalar
        def _(act):
            def embed_copy(t, q):
                lo, hi = BATCHES[q]
                act.wait_ge(emb_tp, at_least(t * 4 + q + 1))
                act.wait_ge(y0_ready, at_least((t - 1) * CHUNKS + 2 * q + 3))
                nc.scalar.copy(emb_t[:, lo * P:hi * P], p_emb[:, 0:(hi - lo) * P]).then_inc(emb_ready, 1)

            def x_root(t):
                act.wait_ge(x_step, at_least(t * 3 + 2))
                nc.scalar.activation(x_sd[:], x_mv[:, 1:2], ACT.Sqrt, bias=eps[:]).then_inc(x_sd_ready, 1)

            def x_copy(t, b):
                act.wait_ge(xt_tp, at_least(t + 1))
                act.wait_ge(n_ready, at_least((t - 1) * CHUNKS))
                act.wait_ge(sx_mm, at_least(t - 1))
                nc.scalar.activation(x_t[b][:], p_mlp[:, 0:P], ACT.Identity, scale=c("gd"),
                                     bias=c("bd")).then_inc(x_ready, 1)

            act.wait_ge(constants_set, 1)
            act.wait_ge(weights_in, 16 * SMALL_LOADS)
            x_root(0)
            x_copy(0, 0)
            embed_copy(0, 0)
            act.wait_ge(fold_mm, 1)
            nc.scalar.copy(wl_extra[:], p_out[0:EXTRA, :]).then_inc(wl_extra_ready, 1)

            def step(it, b, k):
                t = tile_no(it, b)
                s = t * CHUNKS + k
                if k % 2 == 1 and k < 7 and exists(t):
                    embed_copy(t, (k + 1) // 2)
                if k == 7 and exists(t + 1):
                    embed_copy(t + 1, 0)
                if is_chunk(s):
                    m = k % 2
                    act.wait_ge(y0_ready, at_least(s + 1))
                    for g in range(GPC):
                        last = nc.scalar.activation(y0sq[:, m, g, :], p_y0[m][0:ROWS, g * E:(g + 1) * E], ACT.Square,
                                                    accum_out=ss[:, m, g:g + 1])
                    last.then_inc(ss_ready, 1)
                    act.wait_ge(ss_ready, at_least(s + 1))
                    nc.scalar.activation(sd0[:, m, :], ss[:, m, :], ACT.Sqrt, bias=eps[0:ROWS], scale=1.0 / E
                                         ).then_inc(sd0_ready, 1)
                if is_chunk(s - 1):
                    m = (k - 1) % 2
                    act.wait_ge(y1_ready, at_least(s))
                    act.wait_ge(v1_ready, at_least(s - 1))
                    nc.scalar.activation(y1sq[:].rearrange("e s p -> e (s p)"), p_y1[m][:], ACT.Square
                                         ).then_inc(sq_ready, 1)
                if is_chunk(s - 2):
                    kz, bz = (k - 2) % CHUNKS, b if k >= 2 else 1 - b
                    act.wait_ge(z_ready, at_least(s - 1))
                    if kz == 0:
                        act.wait_ge(zs_in[bz], at_least(it * (16 * ZS_DMAS)))
                    nc.scalar.copy(zt[bz][:, :, GPC * kz:GPC * (kz + 1)].rearrange("p q g -> p g q"),
                                   p_z[:, 0:GPC * ZCOLS].rearrange("p (g q) -> p g q", g=GPC)).then_inc(zt_ready, 1)
                if is_chunk(s - 1):
                    act.wait_ge(v1_ready, at_least(s))
                    nc.scalar.activation(sd1[:], v1[:], ACT.Sqrt, bias=eps[:], scale=1.0 / PROJ
                                         ).then_inc(sd1_ready, 1)
                if k == 1 and exists(t - 2):
                    act.wait_ge(top1_mm, at_least((t - 1) * 2))
                    for mo in range(TOP1 // P):
                        last = nc.scalar.activation(h1[:, mo, :], p_mlp[:, mo * P:(mo + 1) * P], ACT.Relu,
                                                    bias=c("b1", mo))
                    last.then_inc(h1_ready, 1)
                if k == 2 and exists(t - 2):
                    act.wait_ge(top2_mm, at_least(t - 1))
                    for mo in range(TOP2 // P):
                        last = nc.scalar.activation(h2[:, mo, :], p_mlp[:, mo * P:(mo + 1) * P], ACT.Relu,
                                                    bias=c("b2", mo))
                    last.then_inc(h2_ready, 1)
                if k == 3 and exists(t - 2):
                    act.wait_ge(top3_mm, at_least(t - 1))
                    nc.scalar.copy(y_rows[:, t - 2, :], p_mlp[0:1, 0:P]).then_inc(y_ready, 1)
                if k == 4 and exists(t):
                    act.wait_ge(sx_mm, at_least(t + 1))
                    act.wait_ge(out_mm, at_least(t - 1))
                    nc.scalar.activation(zs[b][CONST_ROW:CONST_ROW + 2, ZQ - 1, :],
                                         p_mlp[CONST_ROW:CONST_ROW + 2, 0:P], ACT.Identity,
                                         bias=c("one", 0, CONST_ROW, CONST_ROW + 2)).then_inc(sx_ready, 1)
                if k == 5 and exists(t + 1):
                    x_root(t + 1)
                if k == 6 and exists(t + 1):
                    x_copy(t + 1, 1 - b)
                if k == 6 and exists(t - 1):
                    act.wait_ge(o_step, at_least((t - 1) * 3 + 2))
                    nc.scalar.activation(o_sd[:], o_mv[:, 1:2], ACT.Sqrt, bias=eps[:]).then_inc(o_sd_ready, 1)
                if k == 7 and exists(t - 1):
                    act.wait_ge(z_tp, at_least(t))
                    act.wait_ge(top1_mm, at_least((t - 1) * 2))
                    for kc in range(ZK):
                        last = nc.scalar.activation(z_t[:, kc, :], p_mlp[:, kc * P:(kc + 1) * P], ACT.Identity,
                                                    scale=c("gl", kc), bias=c("bl", kc))
                    last.then_inc(z_t_ready, 1)

            def pair(it):
                for b in range(2):
                    for k in range(CHUNKS):
                        step(it, b, k)

            walk(act, pair)

        @block.vector
        def _(dve):
            def x_norm(t):
                dve.wait_ge(x_mm, at_least(t + 1))
                nc.vector.bn_stats(x_stats[:], p_mlp[:, 0:E]).then_inc(x_step, 1)
                dve.wait_ge(x_step, at_least(t * 3 + 1))
                nc.vector.memset(gate_dve[:], 0.0)
                nc.vector.bn_aggr(x_mv[:], x_stats[:]).then_inc(x_step, 1)
                dve.wait_ge(x_sd_ready, at_least(t + 1))
                nc.vector.reciprocal(x_r[:], x_sd[:]).then_inc(x_step, 1)
                dve.wait_ge(x_step, at_least(t * 3 + 3))
                dve.wait_ge(xt_tp, at_least(t))
                nc.vector.tensor_scalar(xn[:], p_mlp[:, 0:E], x_mv[:, 0:1], x_r[:], ALU.subtract, ALU.mult
                                        ).then_inc(xn_ready, 1)

            def indices(b):
                nc.vector.tensor_tensor(idx[:, b, :], ids_raw[:, b, :], offs[:], ALU.add).then_inc(idx_ready, 1)

            nc.vector.memset(eps[:], EPS)
            nc.vector.memset(gate[:], 0.0)
            nc.vector.memset(ones[:], 1.0)
            nc.vector.memset(zero_one[:, 0:1], 0.0)
            nc.vector.memset(zero_one[:, 1:2], 1.0)
            for m in range(2):
                nc.vector.memset(nbuf[m][:, :, PROJ + 1:ZCOLS], 1.0)
            nc.vector.memset(fold[:], 0.0)
            nc.vector.memset(fold_x[:], 0.0).then_inc(constants_set, 1)
            for b in range(2):
                dve.wait_ge(ids_in[b], 16)
                if b == 0:
                    dve.wait_ge(weights_in, 16 * SMALL_LOADS)
                indices(b)
            nc.vector.reduce_sum(ws_mean[:], ws_sb[:], axis=AX_X).then_inc(mean_step, 1)
            nc.vector.reduce_sum(mix_mean[:], mix_sb[0:ROWS], axis=AX_X).then_inc(mean_step, 1)
            dve.wait_ge(mean_step, 2)
            nc.vector.tensor_scalar(ws_mean[:], ws_mean[:], 1.0 / E, None, ALU.mult).then_inc(mean_step, 1)
            nc.vector.tensor_scalar(mix_mean[:], mix_mean[:], 1.0 / PROJ, None, ALU.mult).then_inc(mean_step, 1)
            dve.wait_ge(mean_step, 4)
            nc.vector.tensor_tensor(ws_sb[:], ws_sb[:], ws_mean[:].unsqueeze(2).to_broadcast([P, 2, E]),
                                    ALU.subtract).then_inc(centred, 1)
            nc.vector.tensor_tensor(mix_sb[0:ROWS], mix_sb[0:ROWS],
                                    mix_mean[:].unsqueeze(2).to_broadcast([ROWS, QUAD, PROJ]),
                                    ALU.subtract).then_inc(centred, 1)
            dve.wait_ge(mix_sum_mm, 1)
            nc.vector.tensor_copy(mix_sum[:], p_mlp[0:1, 0:P]).then_inc(mix_sum_ready, 1)
            x_norm(0)
            dve.wait_ge(late_weights_in, 16 * LATE_LOADS)
            nc.vector.tensor_scalar(pair_gain[:], col[:, where["gq"][0]:where["gq"][1]], c("gp"), 0.5,
                                    ALU.mult, ALU.mult).then_inc(fold_step, 1)
            dve.wait_ge(constants_set, 1)
            nc.vector.tensor_scalar(fold[:, 32:32 + PROJ], delta_sb[:], c("gp"), None, ALU.mult).then_inc(fold_step, 1)
            nc.vector.tensor_scalar(fold[:, CONST_ROW:CONST_ROW + 1], c("bp"), E / 2.0, None, ALU.mult
                                    ).then_inc(fold_step, 1)
            nc.vector.tensor_scalar(fold_x[:, 0:PROJ], delta_sb[0:PROJ, :], c("gp", 0, 0, PROJ), None, ALU.mult)
            nc.vector.tensor_copy(fold_x[:, CONST_ROW + 1:EXTRA], c("bp", 0, 0, PROJ))
            dve.wait_ge(fold_step, 3)
            for cc in range(8):
                last = nc.vector.tensor_scalar(fold_q[:, cc, :], fold[:], c("bq", cc), None, ALU.mult)
            last.then_inc(fold_ready, 1)
            dve.wait_ge(fold_mm, 1)
            for cc in range(8):
                last = nc.vector.tensor_scalar(wl_sb[:, cc, :], wl_sb[:, cc, :], pair_gain[:, cc:cc + 1], None,
                                               ALU.mult)
            last.then_inc(wl_ready, 1)

            def step(it, b, k):
                t = tile_no(it, b)
                s = t * CHUNKS + k
                if is_chunk(s):
                    m = k % 2
                    dve.wait_ge(sd0_ready, at_least(s + 1))
                    nc.vector.reciprocal(r0[:, m, :], sd0[:, m, :]).then_inc(r0_ready, 1)
                    dve.wait_ge(r0_ready, at_least(s + 1))
                    dve.wait_ge(y1_ready, at_least(s - 1))
                    for g in range(GPC):
                        last = nc.vector.scalar_tensor_tensor(y0s[m][0:ROWS, g, :], p_y0[m][0:ROWS, g * E:(g + 1) * E],
                                                              r0[:, m, g:g + 1], gs_sb[:], ALU.mult, ALU.mult)
                    last.then_inc(y0s_ready, 1)
                if is_chunk(s - 1):
                    m = (k - 1) % 2
                    kn, bn = (k - 1) % CHUNKS, b if k >= 1 else 1 - b
                    dve.wait_ge(sq_ready, at_least(s))
                    dve.wait_ge(sd1_ready, at_least(s - 1))
                    nc.vector.reduce_sum(v1[:], y1sq[:], axis=AX_X).then_inc(v1_ready, 1)
                    dve.wait_ge(z_ready, at_least(s - 2))
                    if kn == 0:
                        dve.wait_ge(x_ready, at_least(t + 1 if k >= 1 else t))
                    nc.vector.tensor_copy(
                        nbuf[m][:, :, PROJ].rearrange("e (g j) -> e g j", j=QUAD),
                        x_t[bn][:].rearrange("e (j g) -> e g j", j=QUAD)[:, GPC * kn:GPC * (kn + 1), :])
                    dve.wait_ge(sd1_ready, at_least(s))
                    nc.vector.reciprocal(r1[:], sd1[:]).then_inc(r1_ready, 1)
                    dve.wait_ge(r1_ready, at_least(s))
                    nc.vector.tensor_tensor(nbuf[m][:, :, 0:PROJ],
                                            p_y1[m][:].rearrange("e (s p) -> e s p", p=PROJ),
                                            r1[:].unsqueeze(2).to_broadcast([P, SLOTS, PROJ]), ALU.mult
                                            ).then_inc(n_ready, 1)
                if k == 5 and exists(t + 1):
                    x_norm(t + 1)
                if k == 6 and exists(t + 2):
                    dve.wait_ge(ids_in[b], at_least((it + 2) * 16))
                    dve.wait_ge(emb_tp, at_least(t * 4 + 4))
                    indices(b)
                if k == 6 and exists(t - 1):
                    dve.wait_ge(out_mm, at_least(t))
                    nc.vector.bn_stats(o_stats[:], p_out[:]).then_inc(o_step, 1)
                    dve.wait_ge(o_step, at_least((t - 1) * 3 + 1))
                    nc.vector.memset(gate_dve[:], 0.0)
                    nc.vector.bn_aggr(o_mv[:], o_stats[:]).then_inc(o_step, 1)
                    dve.wait_ge(o_sd_ready, at_least(t))
                    nc.vector.reciprocal(o_r[:], o_sd[:]).then_inc(o_step, 1)
                    dve.wait_ge(o_step, at_least(t * 3))
                    dve.wait_ge(z_tp, at_least(t - 1))
                    nc.vector.tensor_scalar(zn[:], p_out[:, 0:DIMS_IN_USE], o_mv[:, 0:1], o_r[:],
                                            ALU.subtract, ALU.mult).then_inc(zn_ready, 1)

            def pair(it):
                for b in range(2):
                    for k in range(CHUNKS):
                        step(it, b, k)

            walk(dve, pair)


def lay_out(inputs):
    import numpy as np

    a = {k: np.asarray(v) for k, v in inputs.items()}
    tables = [a[f"tbl_{n}"] for n in range(N_TABLES)]
    first = np.cumsum([0] + [x.shape[0] for x in tables[:-1]])
    flat = np.arange(2 * BLOCKS * P).reshape(2 * BLOCKS, P).T
    q = np.arange(PROJ)
    w = {k: a["L0_rec_" + k] for k in ("Wd", "gd", "bd", "Ws", "gs", "bs", "Wsi", "gsi", "bsi", "Wl", "gl", "bl")}
    out = {
        "rows": np.concatenate(tables, axis=0),
        "ids": a["ids"].reshape(TILES, 2 * BLOCKS, P).transpose(0, 2, 1),
        "row_offsets": first[flat % N_TABLES].astype(np.float32),
    }
    d = a["r_dense_t"].reshape(TILES, 2, GROUPS // 2, QUAD, DK, P)
    out["dense"] = d.transpose(0, 5, 4, 3, 2, 1).reshape(TILES, P, DK, P)
    ws = np.zeros((2, D_SPARSE, 2, E), np.float32)
    mix = np.zeros((QUAD, N_TABLES, QUAD, PROJ), np.float32)
    for h in range(2):
        ws[h, :, h, :] = w["Ws"].T
    for j in range(QUAD):
        mix[j, :, j, :] = w["Wsi"].T
    out["ws"] = ws.reshape(P, 2, E)
    out["mix"] = mix.reshape(ROWS, QUAD, PROJ)
    out["bs_row"] = np.tile(w["bs"], GPC).reshape(1, GPC, E)
    out["gs_rows"] = np.tile(w["gs"], (ROWS, 1))
    out["wd"] = w["Wd"].T.reshape(DK, P, E).transpose(1, 0, 2)
    pi, pj = np.tril_indices(PROJ + 1, k=-1)
    pairs = np.zeros((PROJ + 1, PROJ + 1, MAXD), np.float32)
    pairs[pi, pj] = w["Wl"].T
    pairs[pj, pi] = w["Wl"].T
    out["wl_pairs"] = pairs[1:, 1:].reshape(PROJ, 8, QUAD, MAXD).transpose(2, 0, 1, 3).reshape(P, 8, MAXD)
    out["wl_x"] = pairs[1:, 0]
    out["delta"] = np.tile(np.eye(PROJ, dtype=np.float32), (QUAD, 1))
    out["ident"] = np.eye(P, dtype=np.float32)
    by_q = lambda v: np.repeat(v.reshape(8, QUAD).T, PROJ, axis=0)
    down = lambda v: v.reshape(-1, P).T
    out["cols"] = np.concatenate([
        np.tile(w["gsi"], QUAD)[:, None], np.tile(w["bsi"], QUAD)[:, None], by_q(w["gsi"]), by_q(w["bsi"]),
        w["gd"][:, None], w["bd"][:, None], down(w["gl"][:DIMS_IN_USE]), down(w["bl"][:DIMS_IN_USE]),
        down(a["b_top1"]), down(a["b_top2"]), down(a["W_top3"][:, 0]),
        np.eye(P, dtype=np.float32)[:, CONST_ROW:CONST_ROW + 1]], axis=1)
    w1 = np.concatenate([a["W_top1"][:DIMS_IN_USE], a["W_top1"][MAXD:]], axis=0)
    out["w1"] = w1.reshape(ZK + DK, P, TOP1).transpose(1, 0, 2)
    out["w2"] = a["W_top2"].reshape(TOP1 // P, P, TOP2).transpose(1, 0, 2)
    return {k: np.ascontiguousarray(v) for k, v in out.items()}


def kernel(**inputs):
    import numpy as np
    import concourse.bacc as bacc
    from concourse.bass_utils import run_bass_kernel_spmd

    nc = bacc.Bacc("TRN2", target_bir_lowering=False, num_devices=1)
    arrays, args = {}, {}
    for name, a in lay_out(inputs).items():
        arrays[f"in_{name}"] = a
        args[name] = nc.dram_tensor(f"in_{name}", a.shape, mybir.dt.from_np(a.dtype), kind="ExternalInput").ap()
    y = nc.dram_tensor("out_y", (1, TILES, P), F32, kind="ExternalOutput").ap()
    dlrm_tower(nc, *args.values(), y)
    r = run_bass_kernel_spmd(nc, [arrays], core_ids=[0])
    got = np.asarray(r.results[0]["out_y"]).reshape(TILES, QUAD, GROUPS // 2, 2)
    return np.ascontiguousarray(got.transpose(0, 3, 2, 1).reshape(BATCH, 1))
```

```python
from contextlib import ExitStack

import concourse.bass as bass
from concourse import mybir

F32 = mybir.dt.float32
I32 = mybir.dt.int32
F32R = mybir.dt.float32r
ALU = mybir.AluOpType
ACT = mybir.ActivationFunctionType
AX_X = mybir.AxisListType.X

P = 128
BATCH = 2048
N_TABLES = 26
D_SPARSE = 64
D_DENSE = 256
E = 128
PROJ = 32
MAXD = 512
DIMS_IN_USE = 384
TOP1 = 512
TOP2 = 256
EPS = 1e-5

TILES = BATCH // P
QUAD = 4
GROUPS = P // QUAD
CHUNKS = 8
GPC = GROUPS // CHUNKS
SLOTS = GPC * QUAD
ROWS = QUAD * N_TABLES
MIX_K = ROWS + 1
BLOCKS = P * N_TABLES // P // 2
ZCOLS = PROJ + 2
EXTRA = 66
CONST_ROW = 64
ZK = DIMS_IN_USE // P
DK = D_DENSE // P
BATCHES = [(0, 4), (4, 7), (7, 10), (10, 13)]
FIRST_PAIR, LAST_PAIR = 0, TILES // 2 - 1

PAIR_Q = 8
PAIR_CHUNKS = 5
PAIR_PARTS = [(0, 16, 0, 0, 0), (16, 16, 0, 1, 0), (8, 16, 8, 2, 0), (24, 8, 8, 3, 0), (24, 8, 24, 3, 64),
              (16, 16, 16, 4, 0)]
ZQ = PAIR_CHUNKS + 1
PAIR_PARTS.append((0, PROJ, PROJ, PAIR_CHUNKS, 0))
ZS_PARTS = [(0, 3), (3, ZQ)]
ZS_DMAS = [QUAD * sum(lo <= cc < hi for _, _, _, cc, _ in PAIR_PARTS) for lo, hi in ZS_PARTS]
WL_STEPS = {6: (0, 1), 7: (2,), 0: (3, 4, 5)}


def at_least(count):
    return max(count, 0) if isinstance(count, int) else count


def columns():
    at, where = 0, {}
    for name, n in (("gp", PAIR_CHUNKS), ("bp", PAIR_CHUNKS), ("gq", PAIR_CHUNKS), ("bq", PAIR_CHUNKS), ("share", PAIR_CHUNKS), ("gd", 1), ("bd", 1), ("gl", ZK), ("bl", ZK),
                    ("b1", TOP1 // P), ("b2", TOP2 // P), ("w3", TOP2 // P), ("gx", 1), ("bx", 1), ("one", 1)):
        where[name] = (at, at + n)
        at += n
    return where, at


def dlrm_tower(nc, rows, ids, row_offsets, dense, ws, mix, bs_row, gs_rows, wd, wl_pairs, wl_x, pick_p, pick_q, ident,
               cols, w1, w2, y):
    where, n_cols = columns()
    with ExitStack() as ctx:
        def sb(name, shape, dt=F32):
            return ctx.enter_context(nc.sbuf_tensor(name, shape, dt))

        def bank(name):
            return ctx.enter_context(nc.psum_tensor(name, [P, 512], F32))

        def sem(name):
            return ctx.enter_context(nc.semaphore(name))

        col = sb("col_sb", [P, n_cols])
        ident_sb = sb("ident_sb", [P, P])
        pick_p_sb = sb("pick_p_sb", [P, PAIR_CHUNKS, PROJ])
        pick_q_sb = sb("pick_q_sb", [P, PAIR_CHUNKS, PROJ])
        offs = sb("offs_sb", [P, N_TABLES])
        ws_sb = sb("ws_sb", [P, 2, E])
        ws_hi = sb("ws_hi", [P, 2, E], F32R)
        ws_lo = sb("ws_lo", [P, 2, E], F32R)
        ws_mean = sb("ws_mean", [P, 2])
        mix_sb = sb("mix_sb", [MIX_K, QUAD, PROJ])
        mix_mean = sb("mix_mean", [ROWS, QUAD])
        mix_sum = sb("mix_sum", [1, P])
        gs_sb = sb("gs_sb", [ROWS, E])
        wd_sb = sb("wd_sb", [P, DK, E])
        wl_raw = sb("wl_raw", [P, PAIR_CHUNKS, MAXD])
        wl_hi = sb("wl_hi", [P, ZQ, MAXD], F32R)
        wl_lo = sb("wl_lo", [P, ZQ, MAXD], F32R)
        wlx_raw = sb("wlx_raw", [PROJ, MAXD])
        wl_extra = sb("wl_extra", [EXTRA, MAXD])
        gain_p = sb("gain_p", [P, PAIR_CHUNKS])
        offset_p = sb("offset_p", [P, PAIR_CHUNKS])
        pair_gain = sb("pair_gain", [P, PAIR_CHUNKS])
        sum_p = sb("sum_p", [P, PAIR_CHUNKS])
        sum_q = sb("sum_q", [P, PAIR_CHUNKS])
        sum_pq = sb("sum_pq", [P, PAIR_CHUNKS])
        fold_z = sb("fold_z", [P, PAIR_CHUNKS, EXTRA])
        fold_x = sb("fold_x", [PROJ, EXTRA])
        w1_sb = sb("w1_sb", [P, ZK + DK, TOP1])
        w2_sb = sb("w2_sb", [P, TOP1 // P, TOP2])
        ones = sb("ones_sb", [P, 1])
        zero_one = sb("zero_one", [P, 2])
        eps = sb("eps_sb", [P, 1])

        ids_raw = sb("ids_raw", [P, 2, N_TABLES], I32)
        idx = sb("idx_sb", [P, 2, N_TABLES], I32)
        emb = [sb(f"emb{b}", [P, BLOCKS, 2, D_SPARSE]) for b in range(2)]
        gate = sb("gate", [1, 2])
        gate_dve = sb("gate_dve", [1, 1])
        emb_hi = sb("emb_hi", [P, BLOCKS * P], F32R)
        emb_lo = sb("emb_lo", [P, BLOCKS * P], F32R)
        y0sq = sb("y0sq", [ROWS, 2, GPC, E])
        ss = sb("ss_sb", [ROWS, 2, GPC])
        sd0 = sb("sd0_sb", [ROWS, 2, GPC])
        r0 = sb("r0_sb", [ROWS, 2, GPC])
        y0s = [sb(f"y0s{b}", [MIX_K, GPC, E]) for b in range(2)]
        y1sq = sb("y1sq", [P, SLOTS, PROJ])
        v1 = sb("v1_sb", [P, SLOTS])
        sd1 = sb("sd1_sb", [P, SLOTS])
        r1 = sb("r1_sb", [P, SLOTS])
        nbuf = [sb(f"nbuf{b}", [P, SLOTS, ZCOLS]) for b in range(2)]
        zt = [sb(f"zt{b}", [P, ZCOLS, GROUPS]) for b in range(2)]
        zs = [sb(f"zs{b}", [P, ZQ, P]) for b in range(2)]
        dense_x = [sb(f"dense_x{b}", [P, DK, P]) for b in range(2)]
        x_stats = sb("x_stats", [P, 6])
        x_mv = sb("x_mv", [P, 2])
        x_sd = sb("x_sd", [P, 1])
        x_r = sb("x_r", [P, 1])
        xn = sb("xn_sb", [P, E])
        x_t = [sb(f"x_t{b}", [P, P]) for b in range(2)]
        o_stats = sb("o_stats", [P, 6])
        o_mv = sb("o_mv", [P, 2])
        o_sd = sb("o_sd", [P, 1])
        o_r = sb("o_r", [P, 1])
        zn = sb("zn_sb", [P, DIMS_IN_USE])
        zs_hi = sb("zs_hi", [P, ZQ, P], F32R)
        zs_lo = sb("zs_lo", [P, ZQ, P], F32R)
        top_in = sb("top_in", [P, ZK + DK, P])
        h1 = sb("h1_sb", [P, TOP1 // P, P])
        h2 = sb("h2_sb", [P, TOP2 // P, P])
        y_rows = sb("y_rows", [1, TILES, P])

        p_emb = bank("p_emb")
        p_y0 = [bank(f"p_y0_{b}") for b in range(2)]
        p_y1 = [bank(f"p_y1_{b}") for b in range(2)]
        p_z = bank("p_z")
        p_out = bank("p_out")
        p_mlp = bank("p_mlp")

        def c(name, i=0, p0=0, p1=P):
            return col[p0:p1, where[name][0] + i:where[name][0] + i + 1]

        weights_in = sem("weights_in")
        late_weights_in = sem("late_weights_in")
        top_weights_in = sem("top_weights_in")
        mix_sum_in = sem("mix_sum_in")
        ids_in = [sem(f"ids_in{b}") for b in range(2)]
        idx_ready = sem("idx_ready")
        gate_passed = sem("gate_passed")
        rows_in = [[sem(f"rows_in{b}_{i}") for i in range(BLOCKS)] for b in range(2)]
        emb_tp = sem("emb_tp")
        emb_hi_ready = sem("emb_hi_ready")
        emb_lo_ready = sem("emb_lo_ready")
        ws_hi_ready = sem("ws_hi_ready")
        ws_lo_ready = sem("ws_lo_ready")
        y0_ready = sem("y0_ready")
        ss_ready = sem("ss_ready")
        sd0_ready = sem("sd0_ready")
        r0_ready = sem("r0_ready")
        y0s_ready = sem("y0s_ready")
        y1_ready = sem("y1_ready")
        sq_ready = sem("sq_ready")
        v1_ready = sem("v1_ready")
        sd1_ready = sem("sd1_ready")
        r1_ready = sem("r1_ready")
        n_ready = sem("n_ready")
        z_ready = sem("z_ready")
        zt_ready = sem("zt_ready")
        zs_in = [[sem(f"zs_in{b}_{part}") for part in range(2)] for b in range(2)]
        dense_x_in = [sem(f"dense_x_in{b}") for b in range(2)]
        dense_m_in = sem("dense_m_in")
        x_mm = sem("x_mm")
        x_sd_ready = sem("x_sd_ready")
        x_step = sem("x_step")
        xn_ready = sem("xn_ready")
        xt_tp = sem("xt_tp")
        x_ready = sem("x_ready")
        sx_mm = sem("sx_mm")
        sx_ready = sem("sx_ready")
        out_mm = sem("out_mm")
        o_step = sem("o_step")
        o_sd_ready = sem("o_sd_ready")
        zn_ready = sem("zn_ready")
        z_tp = sem("z_tp")
        z_t_ready = sem("z_t_ready")
        top1_mm = sem("top1_mm")
        zs_hi_ready = sem("zs_hi_ready")
        zs_lo_ready = sem("zs_lo_ready")
        h1_ready = sem("h1_ready")
        top2_mm = sem("top2_mm")
        h2_ready = sem("h2_ready")
        top3_mm = sem("top3_mm")
        y_ready = sem("y_ready")
        y_out = sem("y_out")
        constants_set = sem("constants_set")
        mean_step = sem("mean_step")
        centred = sem("centred")
        mix_sum_mm = sem("mix_sum_mm")
        mix_sum_ready = sem("mix_sum_ready")
        fold_step = sem("fold_step")
        fold_ready = sem("fold_ready")
        fold_mm = sem("fold_mm")
        wl_scaled = sem("wl_scaled")
        wl_extra_ready = sem("wl_extra_ready")
        wl_hi_ready = sem("wl_hi_ready")
        wl_lo_ready = sem("wl_lo_ready")

        SMALL_LOADS, LATE_LOADS, TOP_LOADS = 9, 4, 2
        block = ctx.enter_context(nc.Block())

        def tile_no(it, b):
            return it * 2 + b

        def exists(t):
            return 0 <= t < TILES if isinstance(t, int) else True

        def is_chunk(s):
            return 0 <= s < TILES * CHUNKS if isinstance(s, int) else True

        def walk(engine, pair):
            pair(FIRST_PAIR)
            with engine.Fori(FIRST_PAIR + 1, LAST_PAIR) as it:
                pair(it)
            pair(LAST_PAIR)
            pair(LAST_PAIR + 1)

        @block.sync
        def _(sp):
            for b in range(2):
                sp.dma_start(ids_raw[:, b, :], ids[b]).then_inc(ids_in[b], 16)
            sp.dma_start(offs[:], row_offsets).then_inc(weights_in, 16)
            sp.dma_start(ws_sb[:], ws).then_inc(weights_in, 16)
            sp.dma_start(ident_sb[:], ident).then_inc(weights_in, 16)
            sp.dma_start(mix_sb[0:ROWS], mix).then_inc(weights_in, 16)
            sp.dma_start(wd_sb[:], wd).then_inc(weights_in, 16)
            sp.dma_start(dense_x[0][:], dense[0]).then_inc(dense_x_in[0], 16)
            sp.dma_start(col[:], cols).then_inc(weights_in, 16)
            sp.dma_start(gs_sb[:], gs_rows).then_inc(weights_in, 16)
            for b in range(2):
                sp.dma_start(y0s[b][ROWS:MIX_K], bs_row).then_inc(weights_in, 16)
            sp.dma_start(pick_p_sb[:], pick_p).then_inc(late_weights_in, 16)
            sp.dma_start(pick_q_sb[:], pick_q).then_inc(late_weights_in, 16)
            sp.dma_start(wlx_raw[:], wl_x).then_inc(late_weights_in, 16)
            sp.dma_start(wl_raw[:], wl_pairs).then_inc(late_weights_in, 16)
            sp.dma_start(w1_sb[:], w1).then_inc(top_weights_in, 16)
            sp.dma_start(w2_sb[:], w2).then_inc(top_weights_in, 16)
            sp.wait_ge(mix_sum_ready, 1)
            sp.dma_start(mix_sb[ROWS:MIX_K], mix_sum[:].rearrange("o (j p) -> o j p", j=QUAD)).then_inc(mix_sum_in, 16)

            def tile(it, b):
                t = tile_no(it, b)
                if exists(t - 2):
                    sp.wait_ge(top1_mm, at_least((t - 2) * 2))
                    sp.dma_start(top_in[:, ZK:ZK + DK, :], dense[t - 2]).then_inc(dense_m_in, 16)
                if exists(t + 1):
                    sp.wait_ge(x_mm, at_least(t))
                    sp.dma_start(dense_x[1 - b][:], dense[t + 1]).then_inc(dense_x_in[1 - b], 16)
                if exists(t + 2):
                    sp.wait_ge(idx_ready, at_least(t + 1))
                    sp.dma_start(ids_raw[:, b, :], ids[t + 2]).then_inc(ids_in[b], 16)
                if exists(t - 1):
                    sp.wait_ge(zt_ready, at_least(t * CHUNKS))
                    for p0, n_p, q0, cc, row in PAIR_PARTS:
                        n_q = PAIR_Q if cc < PAIR_CHUNKS else 2
                        part = 0 if cc < ZS_PARTS[0][1] else 1
                        for j in range(QUAD):
                            sp.dma_start(zs[1 - b][row:row + n_p * n_q, cc, 32 * j:32 * j + 32],
                                         zt[1 - b][32 * j + p0:32 * j + p0 + n_p, q0:q0 + n_q, :]
                                         ).then_inc(zs_in[1 - b][part], 16)

            def pair(it):
                for b in range(2):
                    tile(it, b)

            walk(sp, pair)
            sp.wait_ge(y_ready, TILES)
            sp.dma_start(y, y_rows[:]).then_inc(y_out, 16)
            sp.wait_ge(y_out, 16)

        @block.gpsimd
        def _(pool):
            def tile(it, b):
                t = tile_no(it, b)
                if not exists(t):
                    return
                pool.wait_ge(constants_set, 1)
                pool.wait_ge(idx_ready, at_least(t + 1))
                pool.wait_ge(gate_passed, at_least(t))
                nc.gpsimd.tensor_tensor(gate[:, 1:2], gate[:, 0:1], gate[:, 0:1], ALU.add).then_inc(gate_passed, 1)
                for i in range(BLOCKS):
                    for h in range(2):
                        blk = h * BLOCKS + i
                        nc.gpsimd.indirect_dma_start(
                            emb[b][:, i, h, :], None, rows,
                            bass.IndirectOffsetOnAxis(ap=idx[:, b, blk:blk + 1], axis=0),
                        ).then_inc(rows_in[b][i], 16)

            def pair(it):
                for b in range(2):
                    tile(it, b)

            walk(pool, pair)

        @block.tensor
        def _(pe):
            def embed_transposes(t, b, q):
                lo, hi = BATCHES[q]
                pe.wait_ge(emb_lo_ready, at_least(t * 4 + q))
                for i in range(lo, hi):
                    pe.wait_ge(rows_in[b][i], at_least((t - b) * 16 + 32))
                    last = nc.tensor.transpose(p_emb[:, (i - lo) * P:(i - lo + 1) * P],
                                               emb[b][:, i, :, :].rearrange("p h d -> p (h d)"), ident_sb[:])
                last.then_inc(emb_tp, 1)

            def x_matmul(t, b):
                pe.wait_ge(dense_x_in[b], at_least((t - b) * 8 + 16))
                pe.wait_ge(y_ready, at_least(t - 2))
                for kc in range(DK):
                    last = nc.tensor.matmul(p_mlp[:, 0:E], dense_x[b][:, kc, :], wd_sb[:, kc, :],
                                            start=kc == 0, stop=kc == DK - 1)
                last.then_inc(x_mm, 1)

            def fold_matmul():
                pe.wait_ge(late_weights_in, 16 * LATE_LOADS)
                pe.wait_ge(fold_ready, 1)
                for cc in range(PAIR_CHUNKS):
                    nc.tensor.matmul(p_out[0:EXTRA, :], fold_z[:, cc, :], wl_raw[:, cc, :], start=cc == 0, stop=False)
                nc.tensor.matmul(p_out[0:EXTRA, :], fold_x[:], wlx_raw[:], start=False, stop=True).then_inc(fold_mm, 1)

            def wl_matmul(t, k):
                if k == 6:
                    pe.wait_ge(zs_lo_ready, at_least(2 * t + 1))
                    pe.wait_ge(zn_ready, at_least(t))
                    pe.wait_ge(wl_lo_ready, 1)
                if k == 0:
                    pe.wait_ge(zs_lo_ready, at_least(2 * t + 2))
                for cc in WL_STEPS[k]:
                    n = P if cc < PAIR_CHUNKS else EXTRA
                    for z, w in ((zs_hi, wl_hi), (zs_hi, wl_lo), (zs_lo, wl_hi)):
                        last = nc.tensor.matmul(p_out[:], z[0:n, cc, :], w[0:n, cc, :],
                                                start=cc == 0 and z is zs_hi and w is wl_hi,
                                                stop=cc == ZQ - 1 and z is zs_lo)
                if k == 0:
                    last.then_inc(out_mm, 1)

            def x_transpose(t):
                pe.wait_ge(xn_ready, at_least(t + 1))
                nc.tensor.transpose(p_mlp[:, 0:P], xn[:], ident_sb[:]).then_inc(xt_tp, 1)

            pe.wait_ge(centred, 2)
            nc.tensor.matmul(p_mlp[0:1, 0:P], ones[0:ROWS, :], mix_sb[0:ROWS].rearrange("r j p -> r (j p)"),
                             start=True, stop=True).then_inc(mix_sum_mm, 1)
            pe.wait_ge(weights_in, 16 * SMALL_LOADS)
            pe.wait_ge(mix_sum_ready, 1)
            x_matmul(0, 0)
            embed_transposes(0, 0, 0)
            pe.wait_ge(mix_sum_in, 16)
            pe.wait_ge(ws_lo_ready, 1)

            def step(it, b, k):
                t = tile_no(it, b)
                s = t * CHUNKS + k
                if k % 2 == 1 and k < 7 and exists(t):
                    embed_transposes(t, b, (k + 1) // 2)
                if k == 7 and exists(t + 1):
                    embed_transposes(t + 1, 1 - b, 0)
                if is_chunk(s):
                    pe.wait_ge(emb_lo_ready, at_least(t * 4 + k // 2 + 1))
                    pe.wait_ge(y0s_ready, at_least(s - 1))
                    for g2 in range(2):
                        g = 2 * k + g2
                        for x, w in ((emb_hi, ws_hi), (emb_hi, ws_lo), (emb_lo, ws_hi)):
                            last = nc.tensor.matmul(p_y0[k % 2][0:ROWS, g2 * 256:(g2 + 1) * 256],
                                                    x[:, ROWS * g:ROWS * (g + 1)],
                                                    w[:].rearrange("p h e -> p (h e)"),
                                                    start=x is emb_hi and w is ws_hi, stop=x is emb_lo)
                    last.then_inc(y0_ready, 1)
                if is_chunk(s - 1):
                    m = (k - 1) % 2
                    pe.wait_ge(y0s_ready, at_least(s))
                    pe.wait_ge(n_ready, at_least(s - 2))
                    for g in range(GPC):
                        last = nc.tensor.matmul(p_y1[m][:, g * P:(g + 1) * P], y0s[m][:, g, :],
                                                mix_sb[:].rearrange("r j p -> r (j p)"), start=True, stop=True)
                    last.then_inc(y1_ready, 1)
                if is_chunk(s - 3):
                    m = (k - 3) % 2
                    pe.wait_ge(n_ready, at_least(s - 2))
                    pe.wait_ge(zt_ready, at_least(s - 3))
                    for g in range(GPC):
                        for j in range(QUAD):
                            slot = QUAD * g + j
                            last = nc.tensor.matmul(p_z[32 * j:32 * j + 32, g * ZCOLS:(g + 1) * ZCOLS],
                                                    nbuf[m][:, slot, 0:PROJ], nbuf[m][:, slot, :],
                                                    start=True, stop=True, tile_position=(0, 32 * j))
                    last.then_inc(z_ready, 1)
                if k == 0 and exists(t):
                    x_transpose(t)
                if k == 1 and exists(t):
                    pe.wait_ge(x_ready, at_least(t + 1))
                    nc.tensor.matmul(p_mlp[CONST_ROW:CONST_ROW + 2, 0:P], zero_one[:], x_t[b][:],
                                     start=True, stop=True, tile_position=(0, CONST_ROW)).then_inc(sx_mm, 1)
                if k in (6, 7) and exists(t - 1):
                    wl_matmul(t - 1, k)
                if k == 0 and exists(t - 2):
                    wl_matmul(t - 2, k)
                if k == 2 and exists(t - 2):
                    pe.wait_ge(zn_ready, at_least(t - 1))
                    if exists(t):
                        pe.wait_ge(sx_ready, at_least(t + 1))
                    else:
                        pe.wait_ge(y_ready, at_least(t - 2))
                    for kc in range(ZK):
                        last = nc.tensor.transpose(p_mlp[:, kc * P:(kc + 1) * P], zn[:, kc * P:(kc + 1) * P],
                                                   ident_sb[:])
                    last.then_inc(z_tp, 1)
                if k in (3, 4) and exists(t - 2):
                    if k == 3:
                        pe.wait_ge(z_t_ready, at_least(t - 1))
                        pe.wait_ge(dense_m_in, at_least((t - 1) * 16))
                        pe.wait_ge(top_weights_in, 16 * TOP_LOADS)
                    for mo in range(2 * (k - 3), 2 * (k - 3) + 2):
                        for kc in range(ZK + DK):
                            last = nc.tensor.matmul(p_mlp[:, mo * P:(mo + 1) * P], w1_sb[:, kc, mo * P:(mo + 1) * P],
                                                    top_in[:, kc, :], start=kc == 0, stop=kc == ZK + DK - 1)
                    last.then_inc(top1_mm, 1)
                if k == 5 and exists(t - 2):
                    pe.wait_ge(h1_ready, at_least(t - 1))
                    for mo in range(TOP2 // P):
                        for kc in range(TOP1 // P):
                            last = nc.tensor.matmul(p_mlp[:, mo * P:(mo + 1) * P], w2_sb[:, kc, mo * P:(mo + 1) * P],
                                                    h1[:, kc, :], start=kc == 0, stop=kc == TOP1 // P - 1)
                    last.then_inc(top2_mm, 1)
                if k == 6 and exists(t - 2):
                    pe.wait_ge(h2_ready, at_least(t - 1))
                    for kc in range(TOP2 // P):
                        last = nc.tensor.matmul(p_mlp[0:1, 0:P], c("w3", kc), h2[:, kc, :],
                                                start=kc == 0, stop=kc == TOP2 // P - 1)
                    last.then_inc(top3_mm, 1)
                if k == 7 and exists(t + 1):
                    x_matmul(t + 1, 1 - b)
                if k == 4 and isinstance(t, int) and t == 0:
                    fold_matmul()

            def pair(it):
                for b in range(2):
                    for k in range(CHUNKS):
                        step(it, b, k)

            walk(pe, pair)

        @block.scalar
        def _(act):
            def embed_copy(t, q):
                lo, hi = BATCHES[q]
                act.wait_ge(emb_tp, at_least(t * 4 + q + 1))
                act.wait_ge(y0_ready, at_least((t - 1) * CHUNKS + 2 * q + 3))
                nc.scalar.copy(emb_hi[:, lo * P:hi * P], p_emb[:, 0:(hi - lo) * P]).then_inc(emb_hi_ready, 1)

            def x_root(t):
                act.wait_ge(x_step, at_least(t * 3 + 2))
                nc.scalar.activation(x_sd[:], x_mv[:, 1:2], ACT.Sqrt, bias=eps[:]).then_inc(x_sd_ready, 1)

            def x_copy(t, b):
                act.wait_ge(xt_tp, at_least(t + 1))
                act.wait_ge(n_ready, at_least((t - 1) * CHUNKS))
                act.wait_ge(sx_mm, at_least(t - 1))
                nc.scalar.activation(x_t[b][:], p_mlp[:, 0:P], ACT.Identity, scale=c("gd"),
                                     bias=c("bd")).then_inc(x_ready, 1)

            act.wait_ge(constants_set, 1)
            act.wait_ge(weights_in, 16 * SMALL_LOADS)
            act.wait_ge(centred, 1)
            nc.scalar.copy(ws_hi[:], ws_sb[:]).then_inc(ws_hi_ready, 1)
            x_root(0)
            embed_copy(0, 0)

            def prepare_weights(k):
                if k == 5:
                    act.wait_ge(fold_mm, 1)
                    nc.scalar.copy(wl_extra[:], p_out[0:EXTRA, :]).then_inc(wl_extra_ready, 1)
                    act.wait_ge(wl_scaled, 1)
                    act.wait_ge(wl_extra_ready, 1)
                    for cc in range(PAIR_CHUNKS):
                        nc.scalar.copy(wl_hi[:, cc, :], wl_raw[:, cc, :])
                    nc.scalar.copy(wl_hi[0:EXTRA, PAIR_CHUNKS, :], wl_extra[:]).then_inc(wl_hi_ready, 1)

            def step(it, b, k):
                t = tile_no(it, b)
                s = t * CHUNKS + k
                if k % 2 == 1 and k < 7 and exists(t):
                    embed_copy(t, (k + 1) // 2)
                if k == 7 and exists(t + 1):
                    embed_copy(t + 1, 0)
                if is_chunk(s - 2):
                    act.wait_ge(v1_ready, at_least(s - 1))
                    nc.scalar.activation(sd1[:], v1[:], ACT.Sqrt, bias=eps[:], scale=1.0 / PROJ
                                         ).then_inc(sd1_ready, 1)
                if is_chunk(s):
                    m = k % 2
                    act.wait_ge(y0_ready, at_least(s + 1))
                    for g in range(GPC):
                        last = nc.scalar.activation(y0sq[:, m, g, :], p_y0[m][0:ROWS, g * E:(g + 1) * E], ACT.Square,
                                                    accum_out=ss[:, m, g:g + 1])
                    last.then_inc(ss_ready, 1)
                    act.wait_ge(ss_ready, at_least(s + 1))
                    nc.scalar.activation(sd0[:, m, :], ss[:, m, :], ACT.Sqrt, bias=eps[0:ROWS], scale=1.0 / E
                                         ).then_inc(sd0_ready, 1)
                if is_chunk(s - 1):
                    m = (k - 1) % 2
                    act.wait_ge(y1_ready, at_least(s))
                    nc.scalar.activation(y1sq[:].rearrange("e s p -> e (s p)"), p_y1[m][:], ACT.Square
                                         ).then_inc(sq_ready, 1)
                if is_chunk(s - 3):
                    kz, bz = (k - 3) % CHUNKS, b if k >= 3 else 1 - b
                    act.wait_ge(z_ready, at_least(s - 2))
                    if kz == 0:
                        for part in range(2):
                            act.wait_ge(zs_in[b][part], at_least(it * (16 * ZS_DMAS[part])))
                    nc.scalar.copy(zt[bz][:, :, GPC * kz:GPC * (kz + 1)].rearrange("p q g -> p g q"),
                                   p_z[:, 0:GPC * ZCOLS].rearrange("p (g q) -> p g q", g=GPC)).then_inc(zt_ready, 1)
                if k == 0 and exists(t):
                    x_copy(t, b)
                if k == 1 and exists(t):
                    act.wait_ge(sx_mm, at_least(t + 1))
                    act.wait_ge(zs_lo_ready, at_least(2 * (t - 1)))
                    nc.scalar.activation(zs[b][CONST_ROW:CONST_ROW + 2, ZQ - 1, :],
                                         p_mlp[CONST_ROW:CONST_ROW + 2, 0:P], ACT.Identity,
                                         bias=c("one", 0, CONST_ROW, CONST_ROW + 2)).then_inc(sx_ready, 1)
                if k == 1 and exists(t - 2):
                    act.wait_ge(o_step, at_least((t - 2) * 3 + 2))
                    nc.scalar.activation(o_sd[:], o_mv[:, 1:2], ACT.Sqrt, bias=eps[:]).then_inc(o_sd_ready, 1)
                if k == 2 and exists(t - 2):
                    act.wait_ge(z_tp, at_least(t - 1))
                    for kc in range(ZK):
                        last = nc.scalar.activation(top_in[:, kc, :], p_mlp[:, kc * P:(kc + 1) * P], ACT.Identity,
                                                    scale=c("gl", kc), bias=c("bl", kc))
                    last.then_inc(z_t_ready, 1)
                if k == 4 and exists(t - 2):
                    act.wait_ge(top1_mm, at_least((t - 1) * 2))
                    for mo in range(TOP1 // P):
                        last = nc.scalar.activation(h1[:, mo, :], p_mlp[:, mo * P:(mo + 1) * P], ACT.Relu,
                                                    bias=c("b1", mo))
                    last.then_inc(h1_ready, 1)
                if k in (5, 7) and exists(t - 1):
                    part = 0 if k == 5 else 1
                    lo, hi = ZS_PARTS[part]
                    act.wait_ge(zs_in[1 - b][part], at_least((it + b) * (16 * ZS_DMAS[part])))
                    if part == 0:
                        act.wait_ge(out_mm, at_least(t - 1))
                    else:
                        act.wait_ge(sx_ready, at_least(t))
                    nc.scalar.copy(zs_hi[:, lo:hi, :], zs[1 - b][:, lo:hi, :]).then_inc(zs_hi_ready, 1)
                if k == 5 and exists(t - 2):
                    act.wait_ge(top2_mm, at_least(t - 1))
                    for mo in range(TOP2 // P):
                        last = nc.scalar.activation(h2[:, mo, :], p_mlp[:, mo * P:(mo + 1) * P], ACT.Relu,
                                                    bias=c("b2", mo))
                    last.then_inc(h2_ready, 1)
                if k == 6 and exists(t - 2):
                    act.wait_ge(top3_mm, at_least(t - 1))
                    nc.scalar.copy(y_rows[:, t - 2, :], p_mlp[0:1, 0:P]).then_inc(y_ready, 1)
                if k == 7 and exists(t + 1):
                    x_root(t + 1)
                if isinstance(t, int) and t == 0:
                    prepare_weights(k)

            def pair(it):
                for b in range(2):
                    for k in range(CHUNKS):
                        step(it, b, k)

            walk(act, pair)

        @block.vector
        def _(dve):
            def x_norm(t):
                dve.wait_ge(x_mm, at_least(t + 1))
                nc.vector.bn_stats(x_stats[:], p_mlp[:, 0:E]).then_inc(x_step, 1)
                dve.wait_ge(x_step, at_least(t * 3 + 1))
                nc.vector.memset(gate_dve[:], 0.0)
                nc.vector.bn_aggr(x_mv[:], x_stats[:]).then_inc(x_step, 1)
                dve.wait_ge(x_sd_ready, at_least(t + 1))
                nc.vector.reciprocal(x_r[:], x_sd[:]).then_inc(x_step, 1)
                dve.wait_ge(x_step, at_least(t * 3 + 3))
                dve.wait_ge(xt_tp, at_least(t))
                nc.vector.tensor_scalar(xn[:], p_mlp[:, 0:E], x_mv[:, 0:1], x_r[:], ALU.subtract, ALU.mult
                                        ).then_inc(xn_ready, 1)

            def embed_rest(t, q):
                lo, hi = BATCHES[q]
                dve.wait_ge(emb_hi_ready, at_least(t * 4 + q + 1))
                nc.vector.tensor_tensor(emb_lo[:, lo * P:hi * P], p_emb[:, 0:(hi - lo) * P],
                                        emb_hi[:, lo * P:hi * P].bitcast(F32), ALU.subtract).then_inc(emb_lo_ready, 1)

            def indices(b):
                nc.vector.tensor_tensor(idx[:, b, :], ids_raw[:, b, :], offs[:], ALU.add).then_inc(idx_ready, 1)

            nc.vector.memset(eps[:], EPS)
            nc.vector.memset(gate[:], 0.0)
            nc.vector.memset(ones[:], 1.0)
            nc.vector.memset(zero_one[:, 0:1], 0.0)
            nc.vector.memset(zero_one[:, 1:2], 1.0)
            for m in range(2):
                nc.vector.memset(nbuf[m][:, :, PROJ + 1:ZCOLS], 1.0)
            nc.vector.memset(fold_z[:], 0.0)
            for b in range(2):
                nc.vector.memset(zs[b][:, ZQ - 1, :], 0.0)
            nc.vector.memset(fold_x[:], 0.0).then_inc(constants_set, 1)
            for b in range(2):
                dve.wait_ge(ids_in[b], 16)
                if b == 0:
                    dve.wait_ge(weights_in, 16 * SMALL_LOADS)
                indices(b)
            nc.vector.reduce_sum(ws_mean[:], ws_sb[:], axis=AX_X).then_inc(mean_step, 1)
            nc.vector.reduce_sum(mix_mean[:], mix_sb[0:ROWS], axis=AX_X).then_inc(mean_step, 1)
            dve.wait_ge(mean_step, 2)
            nc.vector.tensor_scalar(ws_mean[:], ws_mean[:], 1.0 / E, None, ALU.mult).then_inc(mean_step, 1)
            nc.vector.tensor_scalar(mix_mean[:], mix_mean[:], 1.0 / PROJ, None, ALU.mult).then_inc(mean_step, 1)
            dve.wait_ge(mean_step, 4)
            nc.vector.tensor_tensor(ws_sb[:], ws_sb[:], ws_mean[:].unsqueeze(2).to_broadcast([P, 2, E]),
                                    ALU.subtract).then_inc(centred, 1)
            nc.vector.tensor_tensor(mix_sb[0:ROWS], mix_sb[0:ROWS],
                                    mix_mean[:].unsqueeze(2).to_broadcast([ROWS, QUAD, PROJ]),
                                    ALU.subtract).then_inc(centred, 1)
            dve.wait_ge(ws_hi_ready, 1)
            nc.vector.tensor_tensor(ws_lo[:], ws_sb[:], ws_hi[:].bitcast(F32), ALU.subtract).then_inc(ws_lo_ready, 1)
            dve.wait_ge(mix_sum_mm, 1)
            nc.vector.tensor_copy(mix_sum[:], p_mlp[0:1, 0:P]).then_inc(mix_sum_ready, 1)
            x_norm(0)
            embed_rest(0, 0)

            def prepare_weights(k):
                share = col[:, where["share"][0]:where["share"][1]]
                gq = col[:, where["gq"][0]:where["gq"][1]]
                bq = col[:, where["bq"][0]:where["bq"][1]]
                if k == 2:
                    nc.vector.tensor_tensor(gain_p[:], col[:, where["gp"][0]:where["gp"][1]], share, ALU.mult
                                            ).then_inc(fold_step, 1)
                    nc.vector.tensor_tensor(offset_p[:], col[:, where["bp"][0]:where["bp"][1]], share, ALU.mult
                                            ).then_inc(fold_step, 1)
                    dve.wait_ge(fold_step, 2)
                    nc.vector.tensor_tensor(pair_gain[:], gain_p[:], gq, ALU.mult).then_inc(fold_step, 1)
                    nc.vector.tensor_tensor(sum_p[:], gain_p[:], bq, ALU.mult).then_inc(fold_step, 1)
                    nc.vector.tensor_tensor(sum_q[:], offset_p[:], gq, ALU.mult).then_inc(fold_step, 1)
                    nc.vector.tensor_tensor(sum_pq[:], offset_p[:], bq, ALU.mult).then_inc(fold_step, 1)
                    dve.wait_ge(fold_step, 6)
                    dve.wait_ge(late_weights_in, 16 * LATE_LOADS)
                    for cc in range(PAIR_CHUNKS):
                        nc.vector.tensor_scalar(fold_z[:, cc, 1:2 * PROJ:2], pick_p_sb[:, cc, :], sum_p[:, cc:cc + 1],
                                                None, ALU.mult).then_inc(fold_step, 1)
                        nc.vector.tensor_scalar(fold_z[:, cc, CONST_ROW:CONST_ROW + 1], sum_pq[:, cc:cc + 1],
                                                float(E), None, ALU.mult).then_inc(fold_step, 1)
                    dve.wait_ge(fold_step, 6 + 2 * PAIR_CHUNKS)
                    for cc in range(PAIR_CHUNKS):
                        nc.vector.scalar_tensor_tensor(fold_z[:, cc, 1:2 * PROJ:2], pick_q_sb[:, cc, :],
                                                       sum_q[:, cc:cc + 1], fold_z[:, cc, 1:2 * PROJ:2],
                                                       ALU.mult, ALU.add)
                    nc.vector.tensor_scalar(fold_x[:, 0:2 * PROJ:2], ident_sb[0:PROJ, 0:PROJ], c("gx", 0, 0, PROJ),
                                            None, ALU.mult)
                    nc.vector.tensor_copy(fold_x[:, CONST_ROW + 1:EXTRA], c("bx", 0, 0, PROJ)).then_inc(fold_ready, 1)
                if k == 5:
                    dve.wait_ge(fold_mm, 1)
                    for cc in range(PAIR_CHUNKS):
                        last = nc.vector.tensor_scalar(wl_raw[:, cc, :], wl_raw[:, cc, :], pair_gain[:, cc:cc + 1],
                                                       None, ALU.mult)
                    last.then_inc(wl_scaled, 1)
                    dve.wait_ge(wl_scaled, 1)
                    dve.wait_ge(wl_hi_ready, 1)
                    for cc in range(PAIR_CHUNKS):
                        nc.vector.tensor_tensor(wl_lo[:, cc, :], wl_raw[:, cc, :], wl_hi[:, cc, :].bitcast(F32),
                                                ALU.subtract)
                    nc.vector.tensor_tensor(wl_lo[0:EXTRA, PAIR_CHUNKS, :], wl_extra[:],
                                            wl_hi[0:EXTRA, PAIR_CHUNKS, :].bitcast(F32), ALU.subtract
                                            ).then_inc(wl_lo_ready, 1)

            def step(it, b, k):
                t = tile_no(it, b)
                s = t * CHUNKS + k
                if is_chunk(s - 2):
                    m = k % 2
                    kn, bn = (k - 2) % CHUNKS, b if k >= 2 else 1 - b
                    dve.wait_ge(z_ready, at_least(s - 3))
                    if kn == 0:
                        dve.wait_ge(x_ready, at_least(t + 1))
                    nc.vector.tensor_copy(
                        nbuf[m][:, :, PROJ].rearrange("e (g j) -> e g j", j=QUAD),
                        x_t[bn][:].rearrange("e (j g) -> e g j", j=QUAD)[:, GPC * kn:GPC * (kn + 1), :])
                    dve.wait_ge(sd1_ready, at_least(s - 1))
                    nc.vector.reciprocal(r1[:], sd1[:]).then_inc(r1_ready, 1)
                    dve.wait_ge(r1_ready, at_least(s - 1))
                    nc.vector.tensor_tensor(nbuf[m][:, :, 0:PROJ],
                                            p_y1[m][:].rearrange("e (s p) -> e s p", p=PROJ),
                                            r1[:].unsqueeze(2).to_broadcast([P, SLOTS, PROJ]), ALU.mult
                                            ).then_inc(n_ready, 1)
                if k % 2 == 1 and k < 7 and exists(t):
                    embed_rest(t, (k + 1) // 2)
                if k == 7 and exists(t + 1):
                    embed_rest(t + 1, 0)
                if is_chunk(s):
                    m = k % 2
                    dve.wait_ge(sd0_ready, at_least(s + 1))
                    nc.vector.reciprocal(r0[:, m, :], sd0[:, m, :]).then_inc(r0_ready, 1)
                    dve.wait_ge(r0_ready, at_least(s + 1))
                    dve.wait_ge(y1_ready, at_least(s - 1))
                    for g in range(GPC):
                        last = nc.vector.scalar_tensor_tensor(y0s[m][0:ROWS, g, :], p_y0[m][0:ROWS, g * E:(g + 1) * E],
                                                              r0[:, m, g:g + 1], gs_sb[:], ALU.mult, ALU.mult)
                    last.then_inc(y0s_ready, 1)
                if is_chunk(s - 1):
                    dve.wait_ge(sq_ready, at_least(s))
                    nc.vector.reduce_sum(v1[:], y1sq[:], axis=AX_X).then_inc(v1_ready, 1)
                if k == 7 and exists(t + 1):
                    x_norm(t + 1)
                if k == 6 and exists(t + 2):
                    dve.wait_ge(ids_in[b], at_least((it + 2) * 16))
                    dve.wait_ge(emb_tp, at_least(t * 4 + 4))
                    indices(b)
                if k == 1 and exists(t - 2):
                    dve.wait_ge(out_mm, at_least(t - 1))
                    nc.vector.bn_stats(o_stats[:], p_out[:]).then_inc(o_step, 1)
                    dve.wait_ge(o_step, at_least((t - 2) * 3 + 1))
                    nc.vector.memset(gate_dve[:], 0.0)
                    nc.vector.bn_aggr(o_mv[:], o_stats[:]).then_inc(o_step, 1)
                    dve.wait_ge(o_sd_ready, at_least(t - 1))
                    nc.vector.reciprocal(o_r[:], o_sd[:]).then_inc(o_step, 1)
                    dve.wait_ge(o_step, at_least((t - 1) * 3))
                    nc.vector.tensor_scalar(zn[:], p_out[:, 0:DIMS_IN_USE], o_mv[:, 0:1], o_r[:],
                                            ALU.subtract, ALU.mult).then_inc(zn_ready, 1)
                if k in (5, 7) and exists(t - 1):
                    part = 0 if k == 5 else 1
                    lo, hi = ZS_PARTS[part]
                    dve.wait_ge(zs_hi_ready, at_least(2 * (t - 1) + part + 1))
                    nc.vector.tensor_tensor(zs_lo[:, lo:hi, :], zs[1 - b][:, lo:hi, :],
                                            zs_hi[:, lo:hi, :].bitcast(F32), ALU.subtract).then_inc(zs_lo_ready, 1)
                if isinstance(t, int) and t == 0:
                    prepare_weights(k)

            def pair(it):
                for b in range(2):
                    for k in range(CHUNKS):
                        step(it, b, k)

            walk(dve, pair)


def lay_out(inputs):
    import numpy as np

    a = {k: np.asarray(v) for k, v in inputs.items()}
    tables = [a[f"tbl_{n}"] for n in range(N_TABLES)]
    first = np.cumsum([0] + [x.shape[0] for x in tables[:-1]])
    flat = np.arange(2 * BLOCKS * P).reshape(2 * BLOCKS, P).T
    q = np.arange(PROJ)
    w = {k: a["L0_rec_" + k] for k in ("Wd", "gd", "bd", "Ws", "gs", "bs", "Wsi", "gsi", "bsi", "Wl", "gl", "bl")}
    out = {
        "rows": np.concatenate(tables, axis=0),
        "ids": a["ids"].reshape(TILES, 2 * BLOCKS, P).transpose(0, 2, 1),
        "row_offsets": first[flat % N_TABLES].astype(np.float32),
    }
    d = a["r_dense_t"].reshape(TILES, 2, GROUPS // 2, QUAD, DK, P)
    out["dense"] = d.transpose(0, 5, 4, 3, 2, 1).reshape(TILES, P, DK, P)
    ws = np.zeros((2, D_SPARSE, 2, E), np.float32)
    mix = np.zeros((QUAD, N_TABLES, QUAD, PROJ), np.float32)
    for h in range(2):
        ws[h, :, h, :] = w["Ws"].T
    for j in range(QUAD):
        mix[j, :, j, :] = w["Wsi"].T
    out["ws"] = ws.reshape(P, 2, E)
    out["mix"] = mix.reshape(ROWS, QUAD, PROJ)
    out["bs_row"] = np.tile(w["bs"], GPC).reshape(1, GPC, E)
    out["gs_rows"] = np.tile(w["gs"], (ROWS, 1))
    out["wd"] = w["Wd"].T.reshape(DK, P, E).transpose(1, 0, 2)
    pi, pj = np.tril_indices(PROJ + 1, k=-1)
    pairs = np.zeros((PROJ + 1, PROJ + 1, MAXD), np.float32)
    pairs[pi, pj] = w["Wl"].T
    pairs[pj, pi] = w["Wl"].T
    at_p = np.zeros((PAIR_CHUNKS, P), int)
    at_q = np.zeros((PAIR_CHUNKS, P), int)
    for p0, n_p, q0, cc, row in PAIR_PARTS[:-1]:
        pq = np.arange(n_p * PAIR_Q)
        at_p[cc, row:row + len(pq)] = p0 + pq // PAIR_Q
        at_q[cc, row:row + len(pq)] = q0 + pq % PAIR_Q
    share = np.where(at_p // PAIR_Q == at_q // PAIR_Q, 0.5, 1.0).astype(np.float32)
    out["wl_pairs"] = pairs[1:, 1:][at_p, at_q].transpose(1, 0, 2)
    out["wl_x"] = pairs[1:, 0]
    out["pick_p"] = np.eye(PROJ, dtype=np.float32)[at_p].transpose(1, 0, 2)
    out["pick_q"] = np.eye(PROJ, dtype=np.float32)[at_q].transpose(1, 0, 2)
    out["ident"] = np.eye(P, dtype=np.float32)
    down = lambda v: v.reshape(-1, P).T
    out["cols"] = np.concatenate([
        w["gsi"][at_p].T, w["bsi"][at_p].T, w["gsi"][at_q].T, w["bsi"][at_q].T, share.T,
        w["gd"][:, None], w["bd"][:, None], down(w["gl"][:DIMS_IN_USE]), down(w["bl"][:DIMS_IN_USE]),
        down(a["b_top1"]), down(a["b_top2"]), down(a["W_top3"][:, 0]),
        np.tile(w["gsi"], QUAD)[:, None], np.tile(w["bsi"], QUAD)[:, None],
        np.eye(P, dtype=np.float32)[:, CONST_ROW:CONST_ROW + 1]], axis=1)
    w1 = np.concatenate([a["W_top1"][:DIMS_IN_USE], a["W_top1"][MAXD:]], axis=0)
    out["w1"] = w1.reshape(ZK + DK, P, TOP1).transpose(1, 0, 2)
    out["w2"] = a["W_top2"].reshape(TOP1 // P, P, TOP2).transpose(1, 0, 2)
    return {k: np.ascontiguousarray(v) for k, v in out.items()}


def kernel(**inputs):
    import numpy as np
    import concourse.bacc as bacc
    from concourse.bass_utils import run_bass_kernel_spmd

    nc = bacc.Bacc("TRN2", target_bir_lowering=False, num_devices=1)
    arrays, args = {}, {}
    for name, a in lay_out(inputs).items():
        arrays[f"in_{name}"] = a
        args[name] = nc.dram_tensor(f"in_{name}", a.shape, mybir.dt.from_np(a.dtype), kind="ExternalInput").ap()
    y = nc.dram_tensor("out_y", (1, TILES, P), F32, kind="ExternalOutput").ap()
    dlrm_tower(nc, *args.values(), y)
    r = run_bass_kernel_spmd(nc, [arrays], core_ids=[0])
    got = np.asarray(r.results[0]["out_y"]).reshape(TILES, QUAD, GROUPS // 2, 2)
    return np.ascontiguousarray(got.transpose(0, 3, 2, 1).reshape(BATCH, 1))
```

```python
from contextlib import ExitStack

import concourse.bass as bass
from concourse import mybir

F32 = mybir.dt.float32
I32 = mybir.dt.int32
F32R = mybir.dt.float32r
ALU = mybir.AluOpType
ACT = mybir.ActivationFunctionType
AX_X = mybir.AxisListType.X

P = 128
BATCH = 2048
N_TABLES = 26
D_SPARSE = 64
D_DENSE = 256
E = 128
PROJ = 32
MAXD = 512
DIMS_IN_USE = 384
TOP1 = 512
TOP2 = 256
EPS = 1e-5

TILES = BATCH // P
QUAD = 4
GROUPS = P // QUAD
CHUNKS = 8
GPC = GROUPS // CHUNKS
SLOTS = GPC * QUAD
ROWS = QUAD * N_TABLES
MIX_K = ROWS + 1
BLOCKS = P * N_TABLES // P // 2
ZCOLS = PROJ + 2
EXTRA = 66
CONST_ROW = 64
ZK = DIMS_IN_USE // P
DK = D_DENSE // P
BATCHES = [(0, 4), (4, 7), (7, 10), (10, 13)]
LAST_PAIR = TILES // 2 - 1

PAIR_Q = 8
PAIR_CHUNKS = 5
PAIR_PARTS = [(0, 16, 0, 0, 0), (16, 16, 0, 1, 0), (8, 16, 8, 2, 0), (24, 8, 8, 3, 0), (24, 8, 24, 3, 64),
              (16, 16, 16, 4, 0)]
ZQ = PAIR_CHUNKS + 1
PAIR_PARTS.append((0, PROJ, PROJ, PAIR_CHUNKS, 0))
ZS_PARTS = [(0, 3), (3, ZQ)]
LAST_ON_POOL = [(j, cc) for j in range(QUAD) for cc in range(ZQ) if j == 3 or (j == 2 and cc >= 3)]
ZS_DMAS = [QUAD * sum(lo <= cc < hi for _, _, _, cc, _ in PAIR_PARTS) for lo, hi in ZS_PARTS]
LAST_POOL_DMAS = [sum(lo <= cc < hi and (j, cc) in LAST_ON_POOL for _, _, _, cc, _ in PAIR_PARTS for j in range(QUAD))
                  for lo, hi in ZS_PARTS]
WL_STEPS = {0: (0, 1), 1: (2, 3), 2: (4, 5)}
TOP1_PAIRS = [(mo, kc) for mo in range(TOP1 // P) for kc in range(ZK + DK)]
TOP1_STEPS = {5: TOP1_PAIRS[:7], 6: TOP1_PAIRS[7:14], 7: TOP1_PAIRS[14:]}


def at_least(count):
    return max(count, 0) if isinstance(count, int) else count


def columns():
    at, where = 0, {}
    for name, n in (("gp", PAIR_CHUNKS), ("bp", PAIR_CHUNKS), ("gq", PAIR_CHUNKS), ("bq", PAIR_CHUNKS), ("share", PAIR_CHUNKS), ("gd", 1), ("bd", 1), ("gl", ZK), ("bl", ZK),
                    ("b1", TOP1 // P), ("b2", TOP2 // P), ("w3", TOP2 // P), ("gx", 1), ("bx", 1), ("one", 1)):
        where[name] = (at, at + n)
        at += n
    return where, at


def dlrm_tower(nc, rows, ids, row_offsets, dense, ws, mix, bs_row, gs_rows, wd, wl_pairs, wl_x, pick_p, pick_q, ident,
               cols, w1, w2, y):
    where, n_cols = columns()
    with ExitStack() as ctx:
        def sb(name, shape, dt=F32):
            return ctx.enter_context(nc.sbuf_tensor(name, shape, dt))

        def bank(name):
            return ctx.enter_context(nc.psum_tensor(name, [P, 512], F32))

        def sem(name):
            return ctx.enter_context(nc.semaphore(name))

        col = sb("col_sb", [P, n_cols])
        ident_sb = sb("ident_sb", [P, P])
        pick_p_sb = sb("pick_p_sb", [P, PAIR_CHUNKS, PROJ])
        pick_q_sb = sb("pick_q_sb", [P, PAIR_CHUNKS, PROJ])
        offs = sb("offs_sb", [P, N_TABLES])
        ws_sb = sb("ws_sb", [P, 2, E])
        ws_hi = sb("ws_hi", [P, 2, E], F32R)
        ws_lo = sb("ws_lo", [P, 2, E], F32R)
        ws_mean = sb("ws_mean", [P, 2])
        mix_sb = sb("mix_sb", [MIX_K, QUAD, PROJ])
        mix_mean = sb("mix_mean", [ROWS, QUAD])
        mix_sum = sb("mix_sum", [1, P])
        gs_sb = sb("gs_sb", [ROWS, E])
        wd_sb = sb("wd_sb", [P, DK, E])
        wl_raw = sb("wl_raw", [P, PAIR_CHUNKS, MAXD])
        wl_hi = sb("wl_hi", [P, ZQ, MAXD], F32R)
        wl_lo = sb("wl_lo", [P, ZQ, MAXD], F32R)
        wlx_raw = sb("wlx_raw", [PROJ, MAXD])
        wl_extra = sb("wl_extra", [EXTRA, MAXD])
        gain_p = sb("gain_p", [P, PAIR_CHUNKS])
        offset_p = sb("offset_p", [P, PAIR_CHUNKS])
        pair_gain = sb("pair_gain", [P, PAIR_CHUNKS])
        sum_p = sb("sum_p", [P, PAIR_CHUNKS])
        sum_q = sb("sum_q", [P, PAIR_CHUNKS])
        sum_pq = sb("sum_pq", [P, PAIR_CHUNKS])
        fold_z = sb("fold_z", [P, PAIR_CHUNKS, EXTRA])
        fold_x = sb("fold_x", [PROJ, EXTRA])
        w1_sb = sb("w1_sb", [P, ZK + DK, TOP1])
        w2_sb = sb("w2_sb", [P, TOP1 // P, TOP2])
        ones = sb("ones_sb", [P, 1])
        zero_one = sb("zero_one", [P, 2])
        eps = sb("eps_sb", [P, 1])

        ids_raw = sb("ids_raw", [P, 2, N_TABLES], I32)
        idx = sb("idx_sb", [P, 2, N_TABLES], I32)
        emb = [sb(f"emb{b}", [P, BLOCKS, 2, D_SPARSE]) for b in range(2)]
        gate = sb("gate", [1, 2])
        table_row = sb("table_row", [P, 1])
        gate_dve = sb("gate_dve", [1, 1])
        emb_hi = sb("emb_hi", [P, BLOCKS * P], F32R)
        emb_lo = sb("emb_lo", [P, BLOCKS * P], F32R)
        y0sq = sb("y0sq", [ROWS, 2, GPC, E])
        ss = sb("ss_sb", [ROWS, 2, GPC])
        sd0 = sb("sd0_sb", [ROWS, 2, GPC])
        r0 = sb("r0_sb", [ROWS, 2, GPC])
        y0s = [sb(f"y0s{b}", [MIX_K, GPC, E]) for b in range(2)]
        y1sq = sb("y1sq", [P, SLOTS, PROJ])
        v1 = sb("v1_sb", [P, SLOTS])
        sd1 = sb("sd1_sb", [P, SLOTS])
        r1 = sb("r1_sb", [P, SLOTS])
        nbuf = [sb(f"nbuf{b}", [P, SLOTS, ZCOLS]) for b in range(2)]
        zt = [sb(f"zt{b}", [P, ZCOLS, GROUPS]) for b in range(2)]
        zs = [sb(f"zs{b}", [P, ZQ, P]) for b in range(2)]
        dense_x = [sb(f"dense_x{b}", [P, DK, P]) for b in range(2)]
        x_stats = sb("x_stats", [P, 6])
        x_mv = sb("x_mv", [P, 2])
        x_sd = sb("x_sd", [P, 1])
        x_r = sb("x_r", [P, 1])
        xn = sb("xn_sb", [P, E])
        x_sums = sb("x_sums", [EXTRA, P])
        x_t = [sb(f"x_t{b}", [P, P]) for b in range(2)]
        o_stats = sb("o_stats", [P, 6])
        o_mv = sb("o_mv", [P, 2])
        o_sd = sb("o_sd", [P, 1])
        o_r = sb("o_r", [P, 1])
        zn = sb("zn_sb", [P, DIMS_IN_USE])
        zs_hi = sb("zs_hi", [P, ZQ, P], F32R)
        zs_lo = sb("zs_lo", [P, ZQ, P], F32R)
        top_in = sb("top_in", [P, ZK + DK, P])
        h1 = sb("h1_sb", [P, TOP1 // P, P])
        h2 = sb("h2_sb", [P, TOP2 // P, P])
        y_rows = sb("y_rows", [1, TILES, P])

        p_emb = bank("p_emb")
        p_y0 = [bank(f"p_y0_{b}") for b in range(2)]
        p_y1 = [bank(f"p_y1_{b}") for b in range(2)]
        p_z = bank("p_z")
        p_out = bank("p_out")
        p_x = p_out[:, 0:P]
        p_mlp = bank("p_mlp")
        last_top1 = p_y0 + p_y1

        def c(name, i=0, p0=0, p1=P):
            return col[p0:p1, where[name][0] + i:where[name][0] + i + 1]

        offs_in = sem("offs_in")
        weights_in = sem("weights_in")
        picks_in = sem("picks_in")
        late_weights_in = sem("late_weights_in")
        top_weights_in = sem("top_weights_in")
        mix_sum_in = sem("mix_sum_in")
        ids_in = [sem(f"ids_in{b}") for b in range(2)]
        idx_ready = sem("idx_ready")
        gate_passed = sem("gate_passed")
        rows_in = [[sem(f"rows_in{b}_{i}") for i in range(BLOCKS)] for b in range(2)]
        emb_tp = sem("emb_tp")
        emb_hi_ready = sem("emb_hi_ready")
        emb_lo_ready = sem("emb_lo_ready")
        ws_hi_ready = sem("ws_hi_ready")
        ws_lo_ready = sem("ws_lo_ready")
        y0_ready = sem("y0_ready")
        ss_ready = sem("ss_ready")
        sd0_ready = sem("sd0_ready")
        r0_ready = sem("r0_ready")
        y0s_ready = sem("y0s_ready")
        y1_ready = sem("y1_ready")
        sq_ready = sem("sq_ready")
        v1_ready = sem("v1_ready")
        sd1_ready = sem("sd1_ready")
        r1_ready = sem("r1_ready")
        n_ready = sem("n_ready")
        z_ready = sem("z_ready")
        zt_ready = sem("zt_ready")
        zs_in = [[sem(f"zs_in{b}_{part}") for part in range(2)] for b in range(2)]
        last_z_in = [sem(f"last_z_in{part}") for part in range(2)]
        dense_x_in = [sem(f"dense_x_in{b}") for b in range(2)]
        dense_m_in = sem("dense_m_in")
        x_mm = sem("x_mm")
        x_sd_ready = sem("x_sd_ready")
        x_step = sem("x_step")
        xn_ready = sem("xn_ready")
        xt_tp = sem("xt_tp")
        x_ready = sem("x_ready")
        sx_mm = sem("sx_mm")
        sx_ready = sem("sx_ready")
        sums_placed = sem("sums_placed")
        out_mm = sem("out_mm")
        o_step = sem("o_step")
        o_sd_ready = sem("o_sd_ready")
        zn_ready = sem("zn_ready")
        z_tp = sem("z_tp")
        z_t_ready = sem("z_t_ready")
        top1_mm = sem("top1_mm")
        zs_hi_ready = sem("zs_hi_ready")
        zs_lo_ready = sem("zs_lo_ready")
        h1_ready = sem("h1_ready")
        top2_mm = sem("top2_mm")
        h2_ready = sem("h2_ready")
        top3_mm = sem("top3_mm")
        y_ready = sem("y_ready")
        y_out = sem("y_out")
        gate_set = sem("gate_set")
        constants_set = sem("constants_set")
        mean_step = sem("mean_step")
        centred = sem("centred")
        mix_sum_mm = sem("mix_sum_mm")
        mix_sum_ready = sem("mix_sum_ready")
        fold_step = sem("fold_step")
        fold_ready = sem("fold_ready")
        fold_mm = sem("fold_mm")
        wl_extra_ready = sem("wl_extra_ready")
        wl_hi_ready = sem("wl_hi_ready")
        wl_lo_ready = sem("wl_lo_ready")

        SMALL_LOADS, LATE_LOADS, TOP_LOADS = 8, 2, 2
        block = ctx.enter_context(nc.Block())

        def tile_no(it, b):
            return it * 2 + b

        def exists(t):
            return 0 <= t < TILES if isinstance(t, int) else True

        def is_chunk(s):
            return 0 <= s < TILES * CHUNKS if isinstance(s, int) else True

        def finishes(t):
            return exists(t) and not (isinstance(t, int) and t == TILES - 2)

        def is_last(t):
            return isinstance(t, int) and t == TILES - 1

        def walk(engine, pair):
            pair(0)
            pair(1)
            with engine.Fori(2, LAST_PAIR) as it:
                pair(it)
            pair(LAST_PAIR)
            pair(LAST_PAIR + 1)
            pair(LAST_PAIR + 2)

        @block.sync
        def _(sp):
            sp.dma_start(ids_raw[:, 0, :], ids[0]).then_inc(ids_in[0], 16)
            sp.dma_start(offs[:], row_offsets).then_inc(offs_in, 16)
            sp.dma_start(ws_sb[:], ws).then_inc(weights_in, 16)
            sp.dma_start(ident_sb[:], ident).then_inc(weights_in, 16)
            sp.dma_start(ids_raw[:, 1, :], ids[1]).then_inc(ids_in[1], 16)
            sp.dma_start(mix_sb[0:ROWS], mix).then_inc(weights_in, 16)
            sp.dma_start(wd_sb[:], wd).then_inc(weights_in, 16)
            sp.dma_start(dense_x[0][:], dense[0]).then_inc(dense_x_in[0], 16)
            sp.dma_start(col[:], cols).then_inc(weights_in, 16)
            sp.dma_start(gs_sb[:], gs_rows).then_inc(weights_in, 16)
            for b in range(2):
                sp.dma_start(y0s[b][ROWS:MIX_K], bs_row).then_inc(weights_in, 16)
            sp.dma_start(pick_p_sb[:], pick_p).then_inc(picks_in, 16)
            sp.dma_start(pick_q_sb[:], pick_q).then_inc(picks_in, 16)
            sp.dma_start(wlx_raw[:], wl_x).then_inc(late_weights_in, 16)
            sp.dma_start(wl_raw[:], wl_pairs).then_inc(late_weights_in, 16)
            sp.dma_start(w1_sb[:], w1).then_inc(top_weights_in, 16)
            sp.dma_start(w2_sb[:], w2).then_inc(top_weights_in, 16)
            sp.wait_ge(mix_sum_ready, 1)
            sp.dma_start(mix_sb[ROWS:MIX_K], mix_sum[:].rearrange("o (j p) -> o j p", j=QUAD)).then_inc(mix_sum_in, 16)

            def tile(it, b):
                t = tile_no(it, b)
                if exists(t - 2):
                    sp.wait_ge(top1_mm, at_least(t - 2))
                    sp.dma_start(top_in[:, ZK:ZK + DK, :], dense[t - 2]).then_inc(dense_m_in, 16)
                if exists(t + 1):
                    sp.wait_ge(x_mm, at_least(t))
                    sp.dma_start(dense_x[1 - b][:], dense[t + 1]).then_inc(dense_x_in[1 - b], 16)
                if exists(t + 2):
                    sp.wait_ge(idx_ready, at_least(t + 1))
                    sp.dma_start(ids_raw[:, b, :], ids[t + 2]).then_inc(ids_in[b], 16)
                if exists(t - 1):
                    sp.wait_ge(zt_ready, at_least(t * CHUNKS))
                    for p0, n_p, q0, cc, row in PAIR_PARTS:
                        n_q = PAIR_Q if cc < PAIR_CHUNKS else 2
                        part = 0 if cc < ZS_PARTS[0][1] else 1
                        for j in range(QUAD):
                            if not exists(t) and (j, cc) in LAST_ON_POOL:
                                continue
                            sp.dma_start(zs[1 - b][row:row + n_p * n_q, cc, 32 * j:32 * j + 32],
                                         zt[1 - b][32 * j + p0:32 * j + p0 + n_p, q0:q0 + n_q, :]
                                         ).then_inc(zs_in[1 - b][part], 16)

            def pair(it):
                for b in range(2):
                    tile(it, b)

            walk(sp, pair)
            sp.wait_ge(y_ready, TILES)
            sp.dma_start(y, y_rows[:]).then_inc(y_out, 16)
            sp.wait_ge(y_out, 16)

        @block.gpsimd
        def _(pool):
            def tile(it, b):
                t = tile_no(it, b)
                if not exists(t):
                    return
                pool.wait_ge(gate_set, 1)
                pool.wait_ge(idx_ready, at_least(t + 1))
                pool.wait_ge(gate_passed, at_least(t))
                nc.gpsimd.tensor_tensor(gate[:, 1:2], gate[:, 0:1], gate[:, 0:1], ALU.add).then_inc(gate_passed, 1)
                for i in range(BLOCKS):
                    for h in range(2):
                        blk = h * BLOCKS + i
                        nc.gpsimd.indirect_dma_start(
                            emb[b][:, i, h, :], None, rows,
                            bass.IndirectOffsetOnAxis(ap=idx[:, b, blk:blk + 1], axis=0),
                        ).then_inc(rows_in[b][i], 16)

            def pair(it):
                for b in range(2):
                    tile(it, b)

            walk(pool, pair)
            pool.wait_ge(zt_ready, TILES * CHUNKS)
            b = (TILES - 1) % 2
            for p0, n_p, q0, cc, row in PAIR_PARTS:
                n_q = PAIR_Q if cc < PAIR_CHUNKS else 2
                part = 0 if cc < ZS_PARTS[0][1] else 1
                for j in range(QUAD):
                    if (j, cc) in LAST_ON_POOL:
                        pool.dma_start(zs[b][row:row + n_p * n_q, cc, 32 * j:32 * j + 32],
                                       zt[b][32 * j + p0:32 * j + p0 + n_p, q0:q0 + n_q, :]
                                       ).then_inc(last_z_in[part], 16)

        @block.tensor
        def _(pe):
            def embed_transposes(t, b, q):
                lo, hi = BATCHES[q]
                pe.wait_ge(emb_lo_ready, at_least(t * 4 + q))
                for i in range(lo, hi):
                    pe.wait_ge(rows_in[b][i], at_least((t - b) * 16 + 32))
                    last = nc.tensor.transpose(p_emb[:, (i - lo) * P:(i - lo + 1) * P],
                                               emb[b][:, i, :, :].rearrange("p h d -> p (h d)"), ident_sb[:])
                last.then_inc(emb_tp, 1)

            def x_matmul(t, b):
                pe.wait_ge(dense_x_in[b], at_least((t - b) * 8 + 16))
                if not isinstance(t, int) or t >= 3:
                    pe.wait_ge(zn_ready, t - 2)
                elif t == 2:
                    pe.wait_ge(wl_extra_ready, 1)
                for kc in range(DK):
                    last = nc.tensor.matmul(p_x, dense_x[b][:, kc, :], wd_sb[:, kc, :],
                                            start=kc == 0, stop=kc == DK - 1)
                last.then_inc(x_mm, 1)

            def fold_matmul(k):
                if k == 0:
                    pe.wait_ge(late_weights_in, 16 * LATE_LOADS)
                    pe.wait_ge(fold_ready, 1)
                    pe.wait_ge(sx_ready, 2)
                for cc in range(2 * k, min(2 * k + 2, PAIR_CHUNKS)):
                    nc.tensor.matmul(p_out[0:EXTRA, :], fold_z[:, cc, :], wl_raw[:, cc, :], start=cc == 0, stop=False)
                if k == 2:
                    nc.tensor.matmul(p_out[0:EXTRA, :], fold_x[:], wlx_raw[:], start=False, stop=True
                                     ).then_inc(fold_mm, 1)

            def wl_matmul(t, k):
                if k == 0:
                    sums = min(t + 3, TILES) if isinstance(t, int) else t + 3
                    pe.wait_ge(sx_ready, sums)
                    pe.wait_ge(zs_lo_ready, at_least(2 * t + 1))
                    pe.wait_ge(zn_ready, at_least(t))
                    pe.wait_ge(wl_lo_ready, 1)
                if k == 1:
                    pe.wait_ge(zs_lo_ready, at_least(2 * t + 2))
                for cc in WL_STEPS[k]:
                    n = P if cc < PAIR_CHUNKS else EXTRA
                    for z, w in ((zs_hi, wl_hi), (zs_hi, wl_lo), (zs_lo, wl_hi)):
                        last = nc.tensor.matmul(p_out[:], z[0:n, cc, :], w[0:n, cc, :],
                                                start=cc == 0 and z is zs_hi and w is wl_hi,
                                                stop=cc == ZQ - 1 and z is zs_lo)
                if k == 2:
                    last.then_inc(out_mm, 1)

            def x_transpose(t):
                pe.wait_ge(xn_ready, t + 1)
                nc.tensor.transpose(p_x, xn[:], ident_sb[:]).then_inc(xt_tp, 1)

            def x_sum(t, b):
                pe.wait_ge(x_ready, t + 1)
                nc.tensor.matmul(p_out[CONST_ROW:CONST_ROW + 2, 0:P], zero_one[:], x_t[b][:],
                                 start=True, stop=True, tile_position=(0, CONST_ROW)).then_inc(sx_mm, 1)

            pe.wait_ge(centred, 2)
            nc.tensor.matmul(p_mlp[0:1, 0:P], ones[0:ROWS, :], mix_sb[0:ROWS].rearrange("r j p -> r (j p)"),
                             start=True, stop=True).then_inc(mix_sum_mm, 1)
            pe.wait_ge(weights_in, 16 * SMALL_LOADS)
            x_matmul(0, 0)
            x_transpose(0)
            x_sum(0, 0)
            embed_transposes(0, 0, 0)
            pe.wait_ge(mix_sum_in, 16)
            pe.wait_ge(ws_lo_ready, 1)

            def top1_blocks(kcs):
                for mo in range(TOP1 // P):
                    for kc in kcs:
                        last = nc.tensor.matmul(last_top1[mo][:, 0:P], w1_sb[:, kc, mo * P:(mo + 1) * P],
                                                top_in[:, kc, :], start=kc == ZK, stop=kc == ZK - 1)
                return last

            def top2_matmul(t):
                pe.wait_ge(h1_ready, at_least(t + 1))
                for mo in range(TOP2 // P):
                    for kc in range(TOP1 // P):
                        last = nc.tensor.matmul(p_mlp[:, mo * P:(mo + 1) * P], w2_sb[:, kc, mo * P:(mo + 1) * P],
                                                h1[:, kc, :], start=kc == 0, stop=kc == TOP1 // P - 1)
                last.then_inc(top2_mm, 1)

            def top3_matmul(t):
                pe.wait_ge(h2_ready, at_least(t + 1))
                for kc in range(TOP2 // P):
                    last = nc.tensor.matmul(p_mlp[0:1, 0:P], c("w3", kc), h2[:, kc, :],
                                            start=kc == 0, stop=kc == TOP2 // P - 1)
                last.then_inc(top3_mm, 1)

            def z_matmul(s, k):
                m = (k - 3) % 2
                pe.wait_ge(n_ready, at_least(s + 1))
                pe.wait_ge(zt_ready, at_least(s))
                for g in range(GPC):
                    for j in range(QUAD):
                        slot = QUAD * g + j
                        last = nc.tensor.matmul(p_z[32 * j:32 * j + 32, g * ZCOLS:(g + 1) * ZCOLS],
                                                nbuf[m][:, slot, 0:PROJ], nbuf[m][:, slot, :],
                                                start=True, stop=True, tile_position=(0, 32 * j))
                last.then_inc(z_ready, 1)

            def step(it, b, k):
                t = tile_no(it, b)
                s = t * CHUNKS + k
                if k % 2 == 1 and k < 7 and exists(t):
                    embed_transposes(t, b, (k + 1) // 2)
                if k == 7 and exists(t + 1):
                    embed_transposes(t + 1, 1 - b, 0)
                if k == 5 and exists(t - 2):
                    pe.wait_ge(zn_ready, at_least(t - 1))
                    pe.wait_ge(y_ready, at_least(t - 2))
                    for kc in range(ZK):
                        last = nc.tensor.transpose(p_mlp[:, kc * P:(kc + 1) * P], zn[:, kc * P:(kc + 1) * P],
                                                   ident_sb[:])
                    last.then_inc(z_tp, 1)
                if is_chunk(s - 2):
                    m = k % 2
                    pe.wait_ge(y0s_ready, at_least(s - 1))
                    pe.wait_ge(n_ready, at_least(s - 3))
                    for g in range(GPC):
                        last = nc.tensor.matmul(p_y1[m][:, g * P:(g + 1) * P], y0s[m][:, g, :],
                                                mix_sb[:].rearrange("r j p -> r (j p)"), start=True, stop=True)
                    last.then_inc(y1_ready, 1)
                if is_chunk(s):
                    pe.wait_ge(emb_lo_ready, at_least(t * 4 + k // 2 + 1))
                    pe.wait_ge(y0s_ready, at_least(s - 1))
                    for g2 in range(2):
                        g = 2 * k + g2
                        for x, w in ((emb_hi, ws_hi), (emb_hi, ws_lo), (emb_lo, ws_hi)):
                            last = nc.tensor.matmul(p_y0[k % 2][0:ROWS, g2 * 256:(g2 + 1) * 256],
                                                    x[:, ROWS * g:ROWS * (g + 1)],
                                                    w[:].rearrange("p h e -> p (h e)"),
                                                    start=x is emb_hi and w is ws_hi, stop=x is emb_lo)
                    last.then_inc(y0_ready, 1)
                if k == 7 and exists(t + 1):
                    x_sum(t + 1, 1 - b)
                if is_chunk(s - 3) and not exists(t):
                    z_matmul(s - 3, k)
                if k < 3 and exists(t - 2) and not (k == 0 and is_last(t - 2)):
                    wl_matmul(t - 2, k)
                if k == 3 and finishes(t - 3):
                    top2_matmul(t - 3)
                if k == 4 and finishes(t - 3):
                    top3_matmul(t - 3)
                if k >= 5 and exists(t - 2) and not is_last(t - 2):
                    if k == 5:
                        pe.wait_ge(z_t_ready, at_least(t - 1))
                        pe.wait_ge(dense_m_in, at_least((t - 1) * 16))
                        pe.wait_ge(top_weights_in, 16 * TOP_LOADS)
                    for mo, kc in TOP1_STEPS[k]:
                        last = nc.tensor.matmul(p_mlp[:, mo * P:(mo + 1) * P], w1_sb[:, kc, mo * P:(mo + 1) * P],
                                                top_in[:, kc, :], start=kc == 0, stop=kc == ZK + DK - 1)
                    if k == 7:
                        last.then_inc(top1_mm, 1)
                if k == 2 and is_last(t - 2):
                    pe.wait_ge(dense_m_in, TILES * 16)
                    pe.wait_ge(y0s_ready, TILES * CHUNKS)
                    pe.wait_ge(n_ready, TILES * CHUNKS)
                    top1_blocks(range(ZK, ZK + DK))
                if k == 5 and is_last(t - 2):
                    pe.wait_ge(z_t_ready, TILES)
                    top1_blocks(range(ZK)).then_inc(top1_mm, 1)
                if k == 6 and exists(t + 1):
                    x_transpose(t + 1)
                if k == 7 and is_last(t - 1):
                    wl_matmul(TILES - 1, 0)
                    top2_matmul(TILES - 2)
                    top3_matmul(TILES - 2)
                if k < 3 and isinstance(t, int) and t == 1:
                    fold_matmul(k)
                if is_chunk(s - 3) and exists(t):
                    z_matmul(s - 3, k)
                if k == 4 and exists(t + 1):
                    x_matmul(t + 1, 1 - b)

            def pair(it):
                for b in range(2):
                    for k in range(CHUNKS):
                        step(it, b, k)

            walk(pe, pair)

        @block.scalar
        def _(act):
            def embed_copy(t, q):
                lo, hi = BATCHES[q]
                act.wait_ge(emb_tp, at_least(t * 4 + q + 1))
                act.wait_ge(y0_ready, at_least((t - 1) * CHUNKS + 2 * q + 3))
                nc.scalar.copy(emb_hi[:, lo * P:hi * P], p_emb[:, 0:(hi - lo) * P]).then_inc(emb_hi_ready, 1)

            def x_root(t):
                act.wait_ge(x_step, at_least(t * 3 + 2))
                nc.scalar.activation(x_sd[:], x_mv[:, 1:2], ACT.Sqrt, bias=eps[:]).then_inc(x_sd_ready, 1)

            def x_copy(t, b):
                act.wait_ge(xt_tp, at_least(t + 1))
                act.wait_ge(n_ready, at_least((t - 1) * CHUNKS))
                act.wait_ge(sx_mm, at_least(t - 1))
                nc.scalar.activation(x_t[b][:], p_x, ACT.Identity, scale=c("gd"),
                                     bias=c("bd")).then_inc(x_ready, 1)

            def x_sum_copy(t):
                act.wait_ge(sx_mm, t + 1)
                act.wait_ge(sums_placed, at_least(t))
                nc.scalar.activation(x_sums[CONST_ROW:EXTRA, :], p_out[CONST_ROW:EXTRA, 0:P], ACT.Identity,
                                     bias=c("one", 0, CONST_ROW, EXTRA)).then_inc(sx_ready, 1)

            def x_sum_place(t, b):
                act.wait_ge(sx_ready, t + 1)
                act.wait_ge(zs_lo_ready, at_least(2 * (t - 1)))
                nc.scalar.copy(zs[b][CONST_ROW:EXTRA, ZQ - 1, :], x_sums[CONST_ROW:EXTRA, :]).then_inc(sums_placed, 1)

            act.wait_ge(constants_set, 1)
            nc.scalar.activation(table_row[:], eps[:], ACT.Sqrt)
            act.wait_ge(weights_in, 16 * SMALL_LOADS)
            act.wait_ge(centred, 1)
            nc.scalar.copy(ws_hi[:], ws_sb[:]).then_inc(ws_hi_ready, 1)
            x_root(0)
            x_copy(0, 0)
            x_sum_copy(0)
            embed_copy(0, 0)

            def prepare_weights(t, k):
                if t == 0 and 2 <= k < 2 + PAIR_CHUNKS:
                    cc = k - 2
                    act.wait_ge(late_weights_in, 16 * LATE_LOADS)
                    act.wait_ge(fold_ready, 1)
                    nc.scalar.activation(wl_hi[:, cc, :], wl_raw[:, cc, :], ACT.Copy, scale=pair_gain[:, cc:cc + 1]
                                         ).then_inc(wl_hi_ready, 1)
                if t == 1 and k == 3:
                    act.wait_ge(fold_mm, 1)
                    nc.scalar.copy(wl_extra[:], p_out[0:EXTRA, :]).then_inc(wl_extra_ready, 1)
                    act.wait_ge(wl_extra_ready, 1)
                    nc.scalar.copy(wl_hi[0:EXTRA, PAIR_CHUNKS, :], wl_extra[:]).then_inc(wl_hi_ready, 1)

            def h1_relu(t):
                act.wait_ge(top1_mm, at_least(t + 1))
                for mo in range(TOP1 // P):
                    out = last_top1[mo][:, 0:P] if is_last(t) else p_mlp[:, mo * P:(mo + 1) * P]
                    last = nc.scalar.activation(h1[:, mo, :], out, ACT.Relu,
                                                bias=c("b1", mo))
                last.then_inc(h1_ready, 1)

            def h2_relu(t):
                act.wait_ge(top2_mm, at_least(t + 1))
                for mo in range(TOP2 // P):
                    last = nc.scalar.activation(h2[:, mo, :], p_mlp[:, mo * P:(mo + 1) * P], ACT.Relu,
                                                bias=c("b2", mo))
                last.then_inc(h2_ready, 1)

            def y_copy(t):
                act.wait_ge(top3_mm, at_least(t + 1))
                nc.scalar.copy(y_rows[:, t, :], p_mlp[0:1, 0:P]).then_inc(y_ready, 1)

            def z_copy(it, b, k):
                s = tile_no(it, b) * CHUNKS + k
                kz, bz = (k - 3) % CHUNKS, b if k >= 3 else 1 - b
                act.wait_ge(z_ready, at_least(s - 2))
                if kz == 0:
                    for part in range(2):
                        act.wait_ge(zs_in[b][part], at_least(it * (16 * ZS_DMAS[part])))
                nc.scalar.copy(zt[bz][:, :, GPC * kz:GPC * (kz + 1)].rearrange("p q g -> p g q"),
                               p_z[:, 0:GPC * ZCOLS].rearrange("p (g q) -> p g q", g=GPC)).then_inc(zt_ready, 1)

            def step(it, b, k):
                t = tile_no(it, b)
                s = t * CHUNKS + k
                if k % 2 == 1 and k < 7 and exists(t):
                    embed_copy(t, (k + 1) // 2)
                if k == 7 and exists(t + 1):
                    embed_copy(t + 1, 0)
                if k == 5 and exists(t - 2):
                    act.wait_ge(z_tp, at_least(t - 1))
                    for kc in range(ZK):
                        last = nc.scalar.activation(top_in[:, kc, :], p_mlp[:, kc * P:(kc + 1) * P], ACT.Identity,
                                                    scale=c("gl", kc), bias=c("bl", kc))
                    last.then_inc(z_t_ready, 1)
                if is_chunk(s - 2):
                    m = k % 2
                    act.wait_ge(y1_ready, at_least(s - 1))
                    nc.scalar.activation(y1sq[:].rearrange("e s p -> e (s p)"), p_y1[m][:], ACT.Square
                                         ).then_inc(sq_ready, 1)
                if is_chunk(s):
                    m = k % 2
                    act.wait_ge(y0_ready, at_least(s + 1))
                    for g in range(GPC):
                        last = nc.scalar.activation(y0sq[:, m, g, :], p_y0[m][0:ROWS, g * E:(g + 1) * E], ACT.Square,
                                                    accum_out=ss[:, m, g:g + 1])
                    last.then_inc(ss_ready, 1)
                    act.wait_ge(ss_ready, at_least(s + 1))
                    nc.scalar.activation(sd0[:, m, :], ss[:, m, :], ACT.Sqrt, bias=eps[0:ROWS], scale=1.0 / E
                                         ).then_inc(sd0_ready, 1)
                if k == 4 and finishes(t - 3):
                    y_copy(t - 3)
                if is_chunk(s - 2):
                    act.wait_ge(v1_ready, at_least(s - 1))
                    nc.scalar.activation(sd1[:], v1[:], ACT.Sqrt, bias=eps[:], scale=1.0 / PROJ
                                         ).then_inc(sd1_ready, 1)
                if k == 5 and exists(t + 1):
                    x_root(t + 1)
                if k == 3 and exists(t - 2):
                    act.wait_ge(o_step, at_least((t - 2) * 3 + 2))
                    nc.scalar.activation(o_sd[:], o_mv[:, 1:2], ACT.Sqrt, bias=eps[:]).then_inc(o_sd_ready, 1)
                if k == 1 and exists(t):
                    x_sum_place(t, b)
                if is_chunk(s - 3) and not exists(t):
                    z_copy(it, b, k)
                if k == 0 and finishes(t - 3):
                    h1_relu(t - 3)
                if k == 3 and finishes(t - 3):
                    h2_relu(t - 3)
                if k == 7 and is_last(t - 1):
                    h1_relu(TILES - 2)
                    h2_relu(TILES - 2)
                if k in (6, 7) and exists(t - 1):
                    part = k - 6
                    lo, hi = ZS_PARTS[part]
                    if exists(t):
                        act.wait_ge(zs_in[1 - b][part], at_least((it + b) * (16 * ZS_DMAS[part])))
                    else:
                        act.wait_ge(zs_in[1 - b][part], 16 * (TILES // 2 * ZS_DMAS[part] - LAST_POOL_DMAS[part]))
                        act.wait_ge(last_z_in[part], 16 * LAST_POOL_DMAS[part])
                    if part == 0:
                        act.wait_ge(out_mm, at_least(t - 1))
                    else:
                        act.wait_ge(sums_placed, at_least(t))
                    nc.scalar.copy(zs_hi[:, lo:hi, :], zs[1 - b][:, lo:hi, :]).then_inc(zs_hi_ready, 1)
                if k == 7 and is_last(t - 1):
                    y_copy(TILES - 2)
                if k == 6 and exists(t + 1):
                    x_copy(t + 1, 1 - b)
                if k == 7 and exists(t + 1):
                    x_sum_copy(t + 1)
                if is_chunk(s - 3) and exists(t):
                    z_copy(it, b, k)
                if isinstance(t, int) and t < 2:
                    prepare_weights(t, k)

            def pair(it):
                for b in range(2):
                    for k in range(CHUNKS):
                        step(it, b, k)

            walk(act, pair)

        @block.vector
        def _(dve):
            def x_statistics(t):
                dve.wait_ge(x_mm, at_least(t + 1))
                nc.vector.bn_stats(x_stats[:], p_x).then_inc(x_step, 1)
                dve.wait_ge(x_step, at_least(t * 3 + 1))
                nc.vector.memset(gate_dve[:], 0.0)
                nc.vector.bn_aggr(x_mv[:], x_stats[:]).then_inc(x_step, 1)

            def x_norm(t):
                dve.wait_ge(x_sd_ready, at_least(t + 1))
                nc.vector.reciprocal(x_r[:], x_sd[:]).then_inc(x_step, 1)
                dve.wait_ge(x_step, at_least(t * 3 + 3))
                dve.wait_ge(xt_tp, at_least(t))
                nc.vector.tensor_scalar(xn[:], p_x, x_mv[:, 0:1], x_r[:], ALU.subtract, ALU.mult
                                        ).then_inc(xn_ready, 1)

            def out_statistics(t):
                dve.wait_ge(out_mm, at_least(t + 1))
                nc.vector.bn_stats(o_stats[:], p_out[:]).then_inc(o_step, 1)
                dve.wait_ge(o_step, at_least(t * 3 + 1))
                nc.vector.memset(gate_dve[:], 0.0)
                nc.vector.bn_aggr(o_mv[:], o_stats[:]).then_inc(o_step, 1)

            def out_norm(t):
                dve.wait_ge(o_sd_ready, at_least(t + 1))
                nc.vector.reciprocal(o_r[:], o_sd[:]).then_inc(o_step, 1)
                dve.wait_ge(o_step, at_least(t * 3 + 3))
                nc.vector.tensor_scalar(zn[:], p_out[:, 0:DIMS_IN_USE], o_mv[:, 0:1], o_r[:],
                                        ALU.subtract, ALU.mult).then_inc(zn_ready, 1)

            def embed_rest(t, q):
                lo, hi = BATCHES[q]
                dve.wait_ge(emb_hi_ready, at_least(t * 4 + q + 1))
                nc.vector.tensor_tensor(emb_lo[:, lo * P:hi * P], p_emb[:, 0:(hi - lo) * P],
                                        emb_hi[:, lo * P:hi * P].bitcast(F32), ALU.subtract).then_inc(emb_lo_ready, 1)

            def indices(b):
                nc.vector.tensor_tensor(idx[:, b, :], ids_raw[:, b, :], offs[:], ALU.add).then_inc(idx_ready, 1)

            nc.vector.memset(gate[:], 0.0).then_inc(gate_set, 1)
            dve.wait_ge(ids_in[0], 16)
            dve.wait_ge(offs_in, 16)
            indices(0)
            nc.vector.memset(eps[:], EPS)
            nc.vector.memset(ones[:], 1.0)
            nc.vector.memset(zero_one[:, 0:1], 0.0)
            nc.vector.memset(zero_one[:, 1:2], 1.0)
            for m in range(2):
                nc.vector.memset(nbuf[m][:, :, PROJ + 1:ZCOLS], 1.0)
                nc.vector.memset(zs[m][:, ZQ - 1, :], 0.0)
            nc.vector.memset(fold_z[:], 0.0)
            nc.vector.memset(fold_x[:], 0.0).then_inc(constants_set, 1)
            dve.wait_ge(ids_in[1], 16)
            indices(1)
            dve.wait_ge(weights_in, 16 * SMALL_LOADS)
            nc.vector.reduce_sum(ws_mean[:], ws_sb[:], axis=AX_X).then_inc(mean_step, 1)
            nc.vector.reduce_sum(mix_mean[:], mix_sb[0:ROWS], axis=AX_X).then_inc(mean_step, 1)
            dve.wait_ge(mean_step, 2)
            nc.vector.tensor_scalar(ws_mean[:], ws_mean[:], 1.0 / E, None, ALU.mult).then_inc(mean_step, 1)
            nc.vector.tensor_scalar(mix_mean[:], mix_mean[:], 1.0 / PROJ, None, ALU.mult).then_inc(mean_step, 1)
            dve.wait_ge(mean_step, 4)
            nc.vector.tensor_tensor(ws_sb[:], ws_sb[:], ws_mean[:].unsqueeze(2).to_broadcast([P, 2, E]),
                                    ALU.subtract).then_inc(centred, 1)
            nc.vector.tensor_tensor(mix_sb[0:ROWS], mix_sb[0:ROWS],
                                    mix_mean[:].unsqueeze(2).to_broadcast([ROWS, QUAD, PROJ]),
                                    ALU.subtract).then_inc(centred, 1)
            dve.wait_ge(ws_hi_ready, 1)
            nc.vector.tensor_tensor(ws_lo[:], ws_sb[:], ws_hi[:].bitcast(F32), ALU.subtract).then_inc(ws_lo_ready, 1)
            dve.wait_ge(mix_sum_mm, 1)
            nc.vector.tensor_copy(mix_sum[:], p_mlp[0:1, 0:P]).then_inc(mix_sum_ready, 1)

            def fold_gains():
                share = col[:, where["share"][0]:where["share"][1]]
                gq = col[:, where["gq"][0]:where["gq"][1]]
                bq = col[:, where["bq"][0]:where["bq"][1]]
                nc.vector.tensor_tensor(gain_p[:], col[:, where["gp"][0]:where["gp"][1]], share, ALU.mult
                                        ).then_inc(fold_step, 1)
                nc.vector.tensor_tensor(offset_p[:], col[:, where["bp"][0]:where["bp"][1]], share, ALU.mult
                                        ).then_inc(fold_step, 1)
                dve.wait_ge(fold_step, 2)
                nc.vector.tensor_tensor(pair_gain[:], gain_p[:], gq, ALU.mult).then_inc(fold_step, 1)
                nc.vector.tensor_tensor(sum_p[:], gain_p[:], bq, ALU.mult).then_inc(fold_step, 1)
                nc.vector.tensor_tensor(sum_q[:], offset_p[:], gq, ALU.mult).then_inc(fold_step, 1)
                nc.vector.tensor_tensor(sum_pq[:], offset_p[:], bq, ALU.mult).then_inc(fold_step, 1)
                dve.wait_ge(fold_step, 6)
                dve.wait_ge(picks_in, 32)
                for cc in range(PAIR_CHUNKS):
                    nc.vector.tensor_scalar(fold_z[:, cc, 1:2 * PROJ:2], pick_p_sb[:, cc, :], sum_p[:, cc:cc + 1],
                                            None, ALU.mult).then_inc(fold_step, 1)
                    nc.vector.tensor_scalar(fold_z[:, cc, CONST_ROW:CONST_ROW + 1], sum_pq[:, cc:cc + 1],
                                            float(E), None, ALU.mult).then_inc(fold_step, 1)
                dve.wait_ge(fold_step, 6 + 2 * PAIR_CHUNKS)
                for cc in range(PAIR_CHUNKS):
                    nc.vector.scalar_tensor_tensor(fold_z[:, cc, 1:2 * PROJ:2], pick_q_sb[:, cc, :],
                                                   sum_q[:, cc:cc + 1], fold_z[:, cc, 1:2 * PROJ:2],
                                                   ALU.mult, ALU.add)
                nc.vector.tensor_scalar(fold_x[:, 0:2 * PROJ:2], ident_sb[0:PROJ, 0:PROJ], c("gx", 0, 0, PROJ),
                                        None, ALU.mult)
                nc.vector.tensor_copy(fold_x[:, CONST_ROW + 1:EXTRA], c("bx", 0, 0, PROJ)).then_inc(fold_ready, 1)

            def prepare_weights(t, k):
                if t == 0 and 3 <= k < 3 + PAIR_CHUNKS:
                    cc = k - 3
                    dve.wait_ge(wl_hi_ready, cc + 1)
                    nc.vector.scalar_tensor_tensor(wl_lo[:, cc, :], wl_raw[:, cc, :], pair_gain[:, cc:cc + 1],
                                                   wl_hi[:, cc, :].bitcast(F32), ALU.mult, ALU.subtract)
                if t == 1 and k == 4:
                    dve.wait_ge(wl_hi_ready, ZQ)
                    nc.vector.tensor_tensor(wl_lo[0:EXTRA, PAIR_CHUNKS, :], wl_extra[:],
                                            wl_hi[0:EXTRA, PAIR_CHUNKS, :].bitcast(F32), ALU.subtract
                                            ).then_inc(wl_lo_ready, 1)

            x_statistics(0)
            x_norm(0)
            fold_gains()
            embed_rest(0, 0)

            def step(it, b, k):
                t = tile_no(it, b)
                s = t * CHUNKS + k
                if is_chunk(s - 2):
                    dve.wait_ge(sq_ready, at_least(s - 1))
                    nc.vector.reduce_sum(v1[:], y1sq[:], axis=AX_X).then_inc(v1_ready, 1)
                if k % 2 == 1 and k < 7 and exists(t):
                    embed_rest(t, (k + 1) // 2)
                if k == 7 and exists(t + 1):
                    embed_rest(t + 1, 0)
                if k == 3 and exists(t - 2):
                    out_statistics(t - 2)
                if k == 5 and exists(t + 1):
                    x_statistics(t + 1)
                if is_chunk(s):
                    m = k % 2
                    dve.wait_ge(sd0_ready, at_least(s + 1))
                    nc.vector.reciprocal(r0[:, m, :], sd0[:, m, :]).then_inc(r0_ready, 1)
                    dve.wait_ge(r0_ready, at_least(s + 1))
                    dve.wait_ge(y1_ready, at_least(s - 1))
                    for g in range(GPC):
                        last = nc.vector.scalar_tensor_tensor(y0s[m][0:ROWS, g, :], p_y0[m][0:ROWS, g * E:(g + 1) * E],
                                                              r0[:, m, g:g + 1], gs_sb[:], ALU.mult, ALU.mult)
                    last.then_inc(y0s_ready, 1)
                if is_chunk(s - 2):
                    m = k % 2
                    kn, bn = (k - 2) % CHUNKS, b if k >= 2 else 1 - b
                    dve.wait_ge(z_ready, at_least(s - 3))
                    if kn == 0:
                        dve.wait_ge(x_ready, at_least(t + 1))
                    dve.wait_ge(sd1_ready, at_least(s - 1))
                    nc.vector.reciprocal(r1[:], sd1[:]).then_inc(r1_ready, 1)
                    nc.vector.tensor_copy(
                        nbuf[m][:, :, PROJ].rearrange("e (g j) -> e g j", j=QUAD),
                        x_t[bn][:].rearrange("e (j g) -> e g j", j=QUAD)[:, GPC * kn:GPC * (kn + 1), :])
                    dve.wait_ge(r1_ready, at_least(s - 1))
                    nc.vector.tensor_tensor(nbuf[m][:, :, 0:PROJ],
                                            p_y1[m][:].rearrange("e (s p) -> e s p", p=PROJ),
                                            r1[:].unsqueeze(2).to_broadcast([P, SLOTS, PROJ]), ALU.mult
                                            ).then_inc(n_ready, 1)
                if k == 3 and exists(t - 2):
                    out_norm(t - 2)
                if k == 5 and exists(t + 1):
                    x_norm(t + 1)
                if k == 6 and exists(t + 2):
                    dve.wait_ge(ids_in[b], at_least((it + 2) * 16))
                    dve.wait_ge(emb_tp, at_least(t * 4 + 4))
                    indices(b)
                if k in (6, 7) and exists(t - 1):
                    part = k - 6
                    lo, hi = ZS_PARTS[part]
                    dve.wait_ge(zs_hi_ready, at_least(2 * (t - 1) + part + 1))
                    nc.vector.tensor_tensor(zs_lo[:, lo:hi, :], zs[1 - b][:, lo:hi, :],
                                            zs_hi[:, lo:hi, :].bitcast(F32), ALU.subtract).then_inc(zs_lo_ready, 1)
                if isinstance(t, int) and t < 2:
                    prepare_weights(t, k)

            def pair(it):
                for b in range(2):
                    for k in range(CHUNKS):
                        step(it, b, k)

            walk(dve, pair)


def lay_out(inputs):
    import numpy as np

    a = {k: np.asarray(v) for k, v in inputs.items()}
    tables = [a[f"tbl_{n}"] for n in range(N_TABLES)]
    first = np.cumsum([0] + [x.shape[0] for x in tables[:-1]])
    flat = np.arange(2 * BLOCKS * P).reshape(2 * BLOCKS, P).T
    q = np.arange(PROJ)
    w = {k: a["L0_rec_" + k] for k in ("Wd", "gd", "bd", "Ws", "gs", "bs", "Wsi", "gsi", "bsi", "Wl", "gl", "bl")}
    out = {
        "rows": np.concatenate(tables, axis=0),
        "ids": a["ids"].reshape(TILES, 2 * BLOCKS, P).transpose(0, 2, 1),
        "row_offsets": first[flat % N_TABLES].astype(np.float32),
    }
    d = a["r_dense_t"].reshape(TILES, 2, GROUPS // 2, QUAD, DK, P)
    out["dense"] = d.transpose(0, 5, 4, 3, 2, 1).reshape(TILES, P, DK, P)
    ws = np.zeros((2, D_SPARSE, 2, E), np.float32)
    mix = np.zeros((QUAD, N_TABLES, QUAD, PROJ), np.float32)
    for h in range(2):
        ws[h, :, h, :] = w["Ws"].T
    for j in range(QUAD):
        mix[j, :, j, :] = w["Wsi"].T
    out["ws"] = ws.reshape(P, 2, E)
    out["mix"] = mix.reshape(ROWS, QUAD, PROJ)
    out["bs_row"] = np.tile(w["bs"], GPC).reshape(1, GPC, E)
    out["gs_rows"] = np.tile(w["gs"], (ROWS, 1))
    out["wd"] = w["Wd"].T.reshape(DK, P, E).transpose(1, 0, 2)
    pi, pj = np.tril_indices(PROJ + 1, k=-1)
    pairs = np.zeros((PROJ + 1, PROJ + 1, MAXD), np.float32)
    pairs[pi, pj] = w["Wl"].T
    pairs[pj, pi] = w["Wl"].T
    at_p = np.zeros((PAIR_CHUNKS, P), int)
    at_q = np.zeros((PAIR_CHUNKS, P), int)
    for p0, n_p, q0, cc, row in PAIR_PARTS[:-1]:
        pq = np.arange(n_p * PAIR_Q)
        at_p[cc, row:row + len(pq)] = p0 + pq // PAIR_Q
        at_q[cc, row:row + len(pq)] = q0 + pq % PAIR_Q
    share = np.where(at_p // PAIR_Q == at_q // PAIR_Q, 0.5, 1.0).astype(np.float32)
    out["wl_pairs"] = pairs[1:, 1:][at_p, at_q].transpose(1, 0, 2)
    out["wl_x"] = pairs[1:, 0]
    out["pick_p"] = np.eye(PROJ, dtype=np.float32)[at_p].transpose(1, 0, 2)
    out["pick_q"] = np.eye(PROJ, dtype=np.float32)[at_q].transpose(1, 0, 2)
    out["ident"] = np.eye(P, dtype=np.float32)
    down = lambda v: v.reshape(-1, P).T
    out["cols"] = np.concatenate([
        w["gsi"][at_p].T, w["bsi"][at_p].T, w["gsi"][at_q].T, w["bsi"][at_q].T, share.T,
        w["gd"][:, None], w["bd"][:, None], down(w["gl"][:DIMS_IN_USE]), down(w["bl"][:DIMS_IN_USE]),
        down(a["b_top1"]), down(a["b_top2"]), down(a["W_top3"][:, 0]),
        np.tile(w["gsi"], QUAD)[:, None], np.tile(w["bsi"], QUAD)[:, None],
        np.eye(P, dtype=np.float32)[:, CONST_ROW:CONST_ROW + 1]], axis=1)
    w1 = np.concatenate([a["W_top1"][:DIMS_IN_USE], a["W_top1"][MAXD:]], axis=0)
    out["w1"] = w1.reshape(ZK + DK, P, TOP1).transpose(1, 0, 2)
    out["w2"] = a["W_top2"].reshape(TOP1 // P, P, TOP2).transpose(1, 0, 2)
    return {k: np.ascontiguousarray(v) for k, v in out.items()}


def kernel(**inputs):
    import numpy as np
    import concourse.bacc as bacc
    from concourse.bass_utils import run_bass_kernel_spmd

    nc = bacc.Bacc("TRN2", target_bir_lowering=False, num_devices=1)
    arrays, args = {}, {}
    for name, a in lay_out(inputs).items():
        arrays[f"in_{name}"] = a
        args[name] = nc.dram_tensor(f"in_{name}", a.shape, mybir.dt.from_np(a.dtype), kind="ExternalInput").ap()
    y = nc.dram_tensor("out_y", (1, TILES, P), F32, kind="ExternalOutput").ap()
    dlrm_tower(nc, *args.values(), y)
    r = run_bass_kernel_spmd(nc, [arrays], core_ids=[0])
    got = np.asarray(r.results[0]["out_y"]).reshape(TILES, QUAD, GROUPS // 2, 2)
    return np.ascontiguousarray(got.transpose(0, 3, 2, 1).reshape(BATCH, 1))
```
